# Optimizing a Trainium2 kernel written in Bass

```python
import numpy as np
import jax
import jax.numpy as jnp

def _softmax(x, axis=-1):
    return jax.nn.softmax(x, axis=axis)

def _gelu(x):
    return jax.nn.gelu(x, approximate=True)

def _silu(x):
    return jax.nn.silu(x)

def _sigmoid(x):
    return jax.nn.sigmoid(x)

def _layernorm(x, axis=-1, eps=1e-05):
    m = jnp.mean(x, axis=axis, keepdims=True)
    v = jnp.var(x, axis=axis, keepdims=True)
    return (x - m) / jnp.sqrt(v + eps)

def _scatter_add(tgt, idx, src, axis=0):
    return tgt.at[idx].add(src)

def _segment_sum(src, seg, n):
    return jax.ops.segment_sum(src, seg, n)
kernel_name = 'mk_xattn_seq_d2_seqx_r4_2eff22'

def setup_inputs(seed: int=0):
    np.random.seed(seed)
    _w = jnp.asarray

    def _rec_inputs():
        import jax
        import jax.numpy as jnp
        _rk = jax.random.key(seed)
        x = -1.528e-05 + 0.9999 * jax.random.normal(jax.random.fold_in(_rk, 1), (64, 256, 256), jnp.float32)
        _lenS = 256 - jax.random.randint(jax.random.fold_in(_rk, 7), (64,), 0, max(1, 256 // 4) + 1, jnp.int32)
        _lenS2 = 77 - jax.random.randint(jax.random.fold_in(_rk, 8), (64,), 0, max(1, 77 // 4) + 1, jnp.int32)
        _ctx_1024P = jax.random.normal(jax.random.fold_in(_rk, 11), (64, 16, 256), jnp.float32)
        _ctx_1024c = jax.random.dirichlet(jax.random.fold_in(_rk, 511), 0.3 * jnp.ones((16,), jnp.float32), (64, 77))
        _ctx_1024t = jnp.einsum('bsk,bkd->bsd', _ctx_1024c, _ctx_1024P)
        _ctx_1024t = _ctx_1024t * jax.lax.rsqrt(jnp.mean(jnp.square(_ctx_1024t)) + 1e-12) * 0.953939
        ctx_1024 = -0.000520686 + 1.00062 * (_ctx_1024t + 0.3 * jax.random.normal(jax.random.fold_in(_rk, 611), (64, 77, 256), jnp.float32))
        return (x, ctx_1024)
    x, ctx_1024 = _rec_inputs()

    def _L0_xattn_setup():
        import jax, jax.numpy as jnp
        import numpy as np
        HIDDEN_NUMS = 128
        key = jax.random.key(seed)
        k1, k2, k3 = jax.random.split(key, 3)
        B, S, T, H2 = (32, 256, 64, 2 * HIDDEN_NUMS)
        target_hidden_states = jax.random.normal(k1, (B, T, H2), dtype=jnp.float32)
        hidden_states = jax.random.normal(k2, (B, S, H2), dtype=jnp.float32)
        trans_W = jax.random.uniform(k3, (4 * HIDDEN_NUMS, H2), dtype=jnp.float32, minval=-0.01, maxval=0.01)
        trans_b = jnp.zeros((H2,), dtype=jnp.float32)
        return {'target_hidden_states': target_hidden_states, 'hidden_states': hidden_states, 'trans_W': trans_W, 'trans_b': trans_b}
    _L0_xattn_all = _L0_xattn_setup()
    _L0_xattn_in = {k: v for k, v in _L0_xattn_all.items() if k in ('trans_W', 'trans_b')}
    del _L0_xattn_all

    def _L1_xattn_setup():
        import jax, jax.numpy as jnp
        import numpy as np
        NEG = -4294967295.0
        EPS = 1e-08
        H = 4
        L = 3

        def _layer_norm(x, g, b):
            mean = jnp.mean(x, axis=-1, keepdims=True)
            std = jnp.std(x, axis=-1, keepdims=True, ddof=1)
            return g * (x - mean) / (std + EPS) + b

        def _mha_layer(q, k, v, Wq, bq, Wk, bk, Wv, bv, gamma, beta):
            B, Sq, d = q.shape
            Sk = k.shape[1]
            dh = d // H
            Q = jax.nn.relu(q @ Wq + bq)
            K = jax.nn.relu(k @ Wk + bk)
            V = jax.nn.relu(v @ Wv + bv)
            Qh = Q.reshape(B, Sq, H, dh).transpose(2, 0, 1, 3)
            Kh = K.reshape(B, Sk, H, dh).transpose(2, 0, 1, 3)
            Vh = V.reshape(B, Sk, H, dh).transpose(2, 0, 1, 3)
            scores = jnp.einsum('hbqd,hbkd->hbqk', Qh, Kh) / jnp.sqrt(jnp.float32(dh))
            key_mask = jnp.sign(jnp.abs(jnp.sum(k, axis=-1)))
            scores = jnp.where(key_mask[None, :, None, :] == 0.0, NEG, scores)
            attn = jax.nn.softmax(scores, axis=-1)
            query_mask = jnp.sign(jnp.abs(jnp.sum(q, axis=-1)))
            attn = attn * query_mask[None, :, :, None]
            out = jnp.einsum('hbqk,hbkd->hbqd', attn, Vh)
            out = out.transpose(1, 2, 0, 3).reshape(B, Sq, d)
            out = out + q
            return _layer_norm(out, gamma, beta)
        key = jax.random.key(seed)
        ks = jax.random.split(key, 8)
        B, S, d = (2, 512, 256)
        inp = {'queries': jax.random.normal(ks[0], (B, S, d), jnp.float32), 'keys': jax.random.normal(ks[1], (B, S, d), jnp.float32), 'values': jax.random.normal(ks[2], (B, S, d), jnp.float32), 'Wq': jax.random.normal(ks[3], (L, d, d), jnp.float32) * 0.02, 'bq': jnp.zeros((L, d), jnp.float32), 'Wk': jax.random.normal(ks[4], (L, d, d), jnp.float32) * 0.02, 'bk': jnp.zeros((L, d), jnp.float32), 'Wv': jax.random.normal(ks[5], (L, d, d), jnp.float32) * 0.02, 'bv': jnp.zeros((L, d), jnp.float32), 'gamma': jnp.ones((L, d), jnp.float32), 'beta': jnp.zeros((L, d), jnp.float32), 'Wff': jax.random.normal(ks[6], (L, d, d), jnp.float32) * 0.02, 'bff': jnp.zeros((L, d), jnp.float32)}
        return inp
    _L1_xattn_all = _L1_xattn_setup()
    _L1_xattn_in = {k: v for k, v in _L1_xattn_all.items() if k in ('Wq', 'bq', 'Wk', 'bk', 'Wv', 'bv', 'gamma', 'beta', 'Wff', 'bff')}
    del _L1_xattn_all
    return {'x': x, 'ctx_1024': ctx_1024, 'L0_xattn_trans_W': _L0_xattn_in['trans_W'], 'L0_xattn_trans_b': _L0_xattn_in['trans_b'], 'L1_xattn_Wq': _L1_xattn_in['Wq'], 'L1_xattn_bq': _L1_xattn_in['bq'], 'L1_xattn_Wk': _L1_xattn_in['Wk'], 'L1_xattn_bk': _L1_xattn_in['bk'], 'L1_xattn_Wv': _L1_xattn_in['Wv'], 'L1_xattn_bv': _L1_xattn_in['bv'], 'L1_xattn_gamma': _L1_xattn_in['gamma'], 'L1_xattn_beta': _L1_xattn_in['beta'], 'L1_xattn_Wff': _L1_xattn_in['Wff'], 'L1_xattn_bff': _L1_xattn_in['bff']}

def reference(x, ctx_1024, L0_xattn_trans_W, L0_xattn_trans_b, L1_xattn_Wq, L1_xattn_bq, L1_xattn_Wk, L1_xattn_bk, L1_xattn_Wv, L1_xattn_bv, L1_xattn_gamma, L1_xattn_beta, L1_xattn_Wff, L1_xattn_bff):
    import jax
    import jax.numpy as jnp

    def _L0_xattn_ref(target_hidden_states, hidden_states, trans_W, trans_b):
        import jax, jax.numpy as jnp
        import numpy as np
        HIDDEN_NUMS = 128
        scores = jnp.einsum('bsd,btd->bst', hidden_states, target_hidden_states)
        attn = jax.nn.softmax(scores, axis=-1)
        ti = jnp.einsum('bst,btd->bsd', attn, target_hidden_states)
        cat = jnp.concatenate([hidden_states, ti], axis=-1)
        hi_new = jnp.tanh(jnp.einsum('bsf,fd->bsd', cat, trans_W) + trans_b)
        return hi_new + hidden_states

    def _L1_xattn_ref(queries, keys, values, Wq, bq, Wk, bk, Wv, bv, gamma, beta, Wff, bff):
        import jax, jax.numpy as jnp
        import numpy as np
        NEG = -4294967295.0
        EPS = 1e-08
        H = 4
        L = 3

        def _layer_norm(x, g, b):
            mean = jnp.mean(x, axis=-1, keepdims=True)
            std = jnp.std(x, axis=-1, keepdims=True, ddof=1)
            return g * (x - mean) / (std + EPS) + b

        def _mha_layer(q, k, v, Wq, bq, Wk, bk, Wv, bv, gamma, beta):
            B, Sq, d = q.shape
            Sk = k.shape[1]
            dh = d // H
            Q = jax.nn.relu(q @ Wq + bq)
            K = jax.nn.relu(k @ Wk + bk)
            V = jax.nn.relu(v @ Wv + bv)
            Qh = Q.reshape(B, Sq, H, dh).transpose(2, 0, 1, 3)
            Kh = K.reshape(B, Sk, H, dh).transpose(2, 0, 1, 3)
            Vh = V.reshape(B, Sk, H, dh).transpose(2, 0, 1, 3)
            scores = jnp.einsum('hbqd,hbkd->hbqk', Qh, Kh) / jnp.sqrt(jnp.float32(dh))
            key_mask = jnp.sign(jnp.abs(jnp.sum(k, axis=-1)))
            scores = jnp.where(key_mask[None, :, None, :] == 0.0, NEG, scores)
            attn = jax.nn.softmax(scores, axis=-1)
            query_mask = jnp.sign(jnp.abs(jnp.sum(q, axis=-1)))
            attn = attn * query_mask[None, :, :, None]
            out = jnp.einsum('hbqk,hbkd->hbqd', attn, Vh)
            out = out.transpose(1, 2, 0, 3).reshape(B, Sq, d)
            out = out + q
            return _layer_norm(out, gamma, beta)
        q, k, v = (queries, keys, values)
        enc = q
        for i in range(L):
            enc = _mha_layer(q, k, v, Wq[i], bq[i], Wk[i], bk[i], Wv[i], bv[i], gamma[i], beta[i])
            enc = jax.nn.leaky_relu(enc @ Wff[i] + bff[i], negative_slope=0.2) + enc
            q, k, v = (enc, enc, enc)
        return enc
    x = _L0_xattn_ref(ctx_1024, x, L0_xattn_trans_W, L0_xattn_trans_b)
    x = _L1_xattn_ref(x, ctx_1024, ctx_1024, L1_xattn_Wq, L1_xattn_bq, L1_xattn_Wk, L1_xattn_bk, L1_xattn_Wv, L1_xattn_bv, L1_xattn_gamma, L1_xattn_beta, L1_xattn_Wff, L1_xattn_bff)
    return x

_drawn_inputs = setup_inputs


def setup_inputs(seed=0):
    import zlib

    import numpy as np

    out = dict(_drawn_inputs(seed))
    spreads = {'L0_xattn_trans_b': (0.0, 0.1),
     'L1_xattn_bq': (0.0, 0.8),
     'L1_xattn_bk': (0.0, 0.8),
     'L1_xattn_bv': (0.0, 0.1),
     'L1_xattn_gamma': (1.0, 0.2),
     'L1_xattn_beta': (0.0, 0.1),
     'L1_xattn_bff': (0.0, 0.1)}
    factors = {'L1_xattn_Wq': 8.0, 'L1_xattn_Wk': 8.0}
    for name, (base, spread) in spreads.items():
        noise = np.random.default_rng([zlib.crc32(name.encode()), seed]).standard_normal(out[name].shape)
        drawn = base * np.exp(spread * noise) if base else spread * noise
        out[name] = jnp.asarray(drawn.astype(out[name].dtype))
    for name, factor in factors.items():
        out[name] = (out[name] * factor).astype(out[name].dtype)
    return out
```

```python
from contextlib import ExitStack

import numpy as np

import concourse.bass as bass
from concourse import mybir

ALU = mybir.AluOpType
ACT = mybir.ActivationFunctionType
AX = mybir.AxisListType
F32 = mybir.dt.float32
F32R = mybir.dt.float32r
BF16 = mybir.dt.bfloat16

P = 128
LAYERS = 3
HEADS = 4
EPS = 1e-8
LEAK = 0.2
COL_BQ, COL_BK, COL_GAMMA, COL_BETA, COL_BFF, COL_BT = 0, 1, 2, 3, 4, 5
HEAD_OF_SLOT = [0, 2, 1, 3]
ISSUE_ORDER = [0, 2, 1, 3]


def build_program(nc, x_t, ctx_t, ctx_n, w_align, w_qkvf, columns, bv_row, identity, out_t):
    batches, D, S = x_t.shape
    T_CTX = ctx_n.shape[1]
    DT = D // P
    ST = S // P
    DH = D // HEADS
    ROUNDS = batches // 2
    CTX_PAD = T_CTX + T_CTX % 2
    VH = DH + 1
    assert D == 2 * P and S == 2 * P and DH == 64 and batches % 2 == 0 and T_CTX < P
    CHAINS = range(2)

    with ExitStack() as ctx:
        def sb(name, shape, dt=F32):
            return ctx.enter_context(nc.sbuf_tensor(name, shape, dt))

        def sb2(name, shape, dt=F32):
            return [sb(f"{name}_{c}", shape, dt) for c in "ab"]

        def sem(name):
            return ctx.enter_context(nc.semaphore(name))

        def sem2(name):
            return [sem(f"{name}_{c}") for c in "ab"]

        stage_w = sb("stage_w", [P, 2, 4, D])
        wa_hi = sb("wa_hi", [P, 2 * DT, D], F32R)
        wa_lo = sb("wa_lo", [P, 2 * DT, D], F32R)
        w_hi = sb("w_hi", [P, LAYERS, 4, DT, D], F32R)
        w_lo = sb("w_lo", [P, LAYERS, 4, DT, D], F32R)
        wk0 = sb("wk0", [P, DT, D])
        cols = sb("cols", [P, 6, LAYERS, DT])
        bq_scaled = sb("bq_scaled", [P, LAYERS, DT])
        ident = sb("ident", [P, P])
        ident_bf = sb("ident_bf", [P, P], BF16)
        ones_f = sb("ones_f", [P, P])
        ones_r = sb("ones_r", [P, P], F32R)
        half = sb("half", [P, ST])
        bv = sb("bv", [P, LAYERS, D])
        bv_hi = sb("bv_hi", [P, LAYERS, D], F32R)
        bv_split = sb("bv_split", [P, LAYERS, D], F32R)

        xt = sb2("xt", [P, DT, S])
        xt_hi = sb2("xt_hi", [P, DT, S], F32R)
        xt_lo = sb2("xt_lo", [P, DT, S], F32R)
        ct = sb2("ct", [P, DT, CTX_PAD])
        ct_hi = sb2("ct_hi", [P, DT, CTX_PAD], F32R)
        ct_lo = sb2("ct_lo", [P, DT, CTX_PAD], F32R)
        cn = sb2("cn", [P, D])
        c_sum = sb2("c_sum", [P, 1])
        c_keep = sb2("c_keep", [P, 1])
        align_nmax = sb2("align_nmax", [P, ST])
        align_sum = sb2("align_sum", [P, ST])
        align_rsum = sb2("align_rsum", [P, ST])
        align_e = sb2("align_e", [P, ST, T_CTX])
        align_p = sb2("align_p", [P, ST, T_CTX])
        align_pt = sb2("align_pt", [P, S])
        cw = sb2("cw", [P, D])
        th = sb2("th", [P, DT, S])
        enc_t = sb2("enc_t", [P, DT, S])
        enc_hi = sb2("enc_hi", [P, DT, S], F32R)
        enc_lo = sb2("enc_lo", [P, DT, S], F32R)
        enc_n = sb2("enc_n", [P, ST, D])
        enc_sum = sb2("enc_sum", [P, ST])
        keep_q = sb2("keep_q", [P, ST])
        keep_k = sb2("keep_k", [P, ST])
        keep_bf = sb2("keep_bf", [P, ST], BF16)
        keep_row = sb2("keep_row", [P, S])
        any_keep = sb2("any_keep", [P, 1])
        none_keep = sb2("none_keep", [P, 1])
        keep_v = sb2("keep_v", [P, ST])
        qt = sb2("qt", [P, DT, S])
        kt_raw = sb2("kt_raw", [P, DT, S])
        kt = sb2("kt", [P, DT, S])
        v = sb2("v", [P, ST, HEADS, VH])
        nmax = sb2("nmax", [P, ST, HEADS])
        prob = sb2("prob", [P, ST, HEADS, S])
        prob_t = sb2("prob_t", [P, HEADS, ST, S])
        rsum = sb2("rsum", [P, ST, HEADS])
        rscale = sb2("rscale", [P, ST, HEADS])
        att = sb2("att", [P, ST, D])
        res = sb2("res", [P, ST, D])
        bn = sb2("bn", [P, ST, 6])
        mv = sb2("mv", [P, ST, 2])
        var = sb2("var", [P, ST])
        std = sb2("std", [P, ST])
        std_eps = sb2("std_eps", [P, ST])
        rstd = sb2("rstd", [P, ST])
        z = sb2("z", [P, ST, D])
        ln_t = sb2("ln_t", [P, DT, S])
        ln_hi = sb2("ln_hi", [P, DT, S], F32R)
        ln_lo = sb2("ln_lo", [P, DT, S], F32R)
        ff = sb2("ff", [P, DT, S])
        ffl = sb2("ffl", [P, DT, S])

        ps = [ctx.enter_context(nc.psum_tensor(f"ps_{c}", [P, 4, 512], F32)) for c in "ab"]

        const_in = sem("const_in")
        w_in = [sem(f"w_in_{n}") for n in range(2)]
        wk0_in = sem("wk0_in")
        w_split = sem("w_split")
        const_rd = sem("const_rd")
        bias_rd = sem("bias_rd")
        pad_rd = sem("pad_rd")
        batch_in = sem2("batch_in")
        out_sent = sem2("out_sent")
        al_sc_mm, al_cw_mm, al_pt_mm, al_x_mm = (sem2(s) for s in ("al_sc_mm", "al_cw_mm", "al_pt_mm", "al_x_mm"))
        nat_mm, q_mm, k_mm, row_mm, v_mm = (sem2(s) for s in ("nat_mm", "q_mm", "k_mm", "row_mm", "v_mm"))
        sc_mm, pt_mm, av_mm, zt_mm, ff_mm = (sem2(s) for s in ("sc_mm", "pt_mm", "av_mm", "zt_mm", "ff_mm"))
        al_e_rd, cw_rd, th_rd = (sem2(s) for s in ("al_e_rd", "cw_rd", "th_rd"))
        nat_rd, q_rd, kraw_rd, v_rd, p_rd = (sem2(s) for s in ("nat_rd", "q_rd", "kraw_rd", "v_rd", "p_rd"))
        pta_rd, lnt_rd, u_rd = (sem2(s) for s in ("pta_rd", "lnt_rd", "u_rd"))
        x_split, ct_split, csum_rd, ckeep_rd = (sem2(s) for s in ("x_split", "ct_split", "csum_rd", "ckeep_rd"))
        al_max_rd, al_rs_rd, al_p_rd, al_pt_rd = (sem2(s) for s in ("al_max_rd", "al_rs_rd", "al_p_rd", "al_pt_rd"))
        keepq_rd, keepk_rd, row_rd, none_rd = (sem2(s) for s in ("keepq_rd", "keepk_rd", "row_rd", "none_rd"))
        keepv_rd, vcol_rd, max_rd, ptd_rd = (sem2(s) for s in ("keepv_rd", "vcol_rd", "max_rd", "ptd_rd"))
        rsum_rd, rscale_rd, att_rd, res_rd, bn_rd = (sem2(s) for s in ("rsum_rd", "rscale_rd", "att_rd", "res_rd", "bn_rd"))
        mv_rd, var_rd, stde_rd, rstd_rd, z_rd = (sem2(s) for s in ("mv_rd", "var_rd", "stde_rd", "rstd_rd", "z_rd"))
        lnhi_rd, ffl_rd, enc_rd, enchi_rd, final_rd = (sem2(s) for s in ("lnhi_rd", "ffl_rd", "enc_rd", "enchi_rd", "final_rd"))
        k_rd, lnlo_rd, enclo_rd = (sem2(s) for s in ("k_rd", "lnlo_rd", "enclo_rd"))
        std_rd = sem2("std_rd")

        def nth(it, l, j=1, per=1):
            return it * (LAYERS * per) + (l * per + j)

        def key_blocks(l):
            return [(0, T_CTX)] if l == 0 else [(s * P, P) for s in range(ST)]

        def bank2(c, b):
            return ps[c][:, b].rearrange("p (m s) -> p m s", m=2)

        BANK_Q, BANK_K, BANK_NATURAL, BANK_ROW = 0, 1, 2, 3
        BANK_V, BANK_ZT, BANK_FF = 0, 0, 3
        BANK_OF_TURN = [1, 2, 0, 3]
        BANK_MIX = 1
        BANK_AL_SCORES, BANK_AL_CW = 1, 2
        BANK_AL_X = [0, 3]

        def run_steps(fori, do):
            A, B = 0, 1

            def tail(c, l, it):
                return [[("center", c, it, l)], [("norm", c, it, l)], [("feed", c, it, l)], [("leak", c, it, l)], [],
                        [("encode", c, it, l)]]

            def align(c, it):
                return [[("align_split", c, it, 0)], [("align_scores", c, it, 0)], [("align_turn", c, it, 0)], [], [],
                        [("align_out", c, it, 0)]]

            def attention(c, l, it, *between):
                for n, names in enumerate((["keys"], ["queries"], ["scores"], ["values"], ["turn_a"], ["turn_b"], ["mix"])):
                    for name in names:
                        do(name, c, it, l)
                    for other in between:
                        for step in other[n] if n < len(other) else []:
                            do(*step)

            def alone(*groups):
                for group in groups:
                    for part in group:
                        for step in part:
                            do(*step)

            def chain_round(it_b, it_a, first, last):
                attention(A, 0, it_a, *([] if first else [tail(B, 0, it_b)]))
                if first:
                    alone(tail(A, 0, it_a))
                else:
                    attention(B, 1, it_b, tail(A, 0, it_a))
                attention(A, 1, it_a, *([] if first else [tail(B, 1, it_b)]))
                if first:
                    alone(tail(A, 1, it_a))
                else:
                    attention(B, 2, it_b, tail(A, 1, it_a))
                attention(A, 2, it_a, *([align(B, it_a)] if first else [tail(B, 2, it_b), align(B, it_a)]))
                attention(B, 0, it_a, *([tail(A, 2, it_a)] if last else [tail(A, 2, it_a), align(A, it_a + 1)]))

            alone(align(A, 0))
            chain_round(None, 0, True, False)
            with fori(0, ROUNDS - 2) as it:
                chain_round(it, it + 1, False, False)
            chain_round(ROUNDS - 2, ROUNDS - 1, False, True)
            alone(tail(B, 0, ROUNDS - 1))
            for l in (1, 2):
                attention(B, l, ROUNDS - 1)
                alone(tail(B, l, ROUNDS - 1))

        block = ctx.enter_context(nc.Block())

        W_LOADS = 1 + LAYERS

        @block.sync
        def _(sp):
            def load(c, b):
                sp.dma_start(xt[c][:], x_t[b].rearrange("(k p) s -> p k s", p=P)).then_inc(batch_in[c], 16)
                sp.dma_start(ct[c][:, :, 0:T_CTX], ctx_t[b].rearrange("(k p) s -> p k s", p=P)).then_inc(batch_in[c], 16)
                sp.dma_start(cn[c][0:T_CTX, :], ctx_n[b]).then_inc(batch_in[c], 16)

            sp.dma_start(cols[:], columns).then_inc(const_in, 16)
            sp.dma_start(ident[:], identity).then_inc(const_in, 16)
            sp.dma_start(bv[0:1], bv_row).then_inc(const_in, 16)
            sp.dma_start(bv[32:33], bv_row).then_inc(const_in, 16)
            sp.dma_start(stage_w[:, 0], w_align.rearrange("(k p) n -> p k n", p=P)).then_inc(w_in[0], 16)
            for c in CHAINS:
                load(c, c)
            n = 1
            for l in range(LAYERS):
                for pair in range(2):
                    if n >= 2:
                        sp.wait_ge(w_split, 2 * (n - 1))
                    sp.dma_start(stage_w[:, n % 2].rearrange("p (w k) n -> p w k n", w=2),
                                 w_qkvf[l, 2 * pair:2 * pair + 2].rearrange("w (k p) n -> p w k n", p=P)).then_inc(w_in[n % 2], 16)
                    n += 1
            sp.dma_start(wk0[:], w_qkvf[0, 1].rearrange("(k p) n -> p k n", p=P)).then_inc(wk0_in, 16)

            def next_batch(c, it):
                sp.wait_ge(enc_rd[c], nth(it, 0))
                sp.wait_ge(k_mm[c], nth(it, 0))
                sp.wait_ge(v_mm[c], nth(it, 0))
                load(c, (it + 1) * 2 + c)

            def store(c, it):
                sp.wait_ge(final_rd[c], it + 1)
                sp.dma_start(out_t[it * 2 + c].rearrange("(k p) s -> p k s", p=P), enc_t[c][:]).then_inc(out_sent[c], 16)

            with sp.Fori(0, ROUNDS - 1) as it:
                for c in CHAINS:
                    next_batch(c, it)
                    store(c, it)
            for c in CHAINS:
                store(c, ROUNDS - 1)
            for c in CHAINS:
                sp.wait_ge(out_sent[c], 16 * ROUNDS)

        @block.tensor
        def _(pe):
            def three(out, a_hi, a_lo, b_hi, b_lo, first, last):
                pe.matmul(out, a_hi, b_hi, start=first, stop=False)
                pe.matmul(out, a_hi, b_lo, start=False, stop=False)
                return pe.matmul(out, a_lo, b_hi, start=False, stop=last)

            def project(out, l, w, hi, lo, blocks=range(DT)):
                for m in blocks:
                    for k in range(DT):
                        mm = three(out[:, m, :], w_hi[:, l, w, k, m * P:(m + 1) * P], w_lo[:, l, w, k, m * P:(m + 1) * P],
                                   hi[:, k, :], lo[:, k, :], k == 0, k == DT - 1)
                return mm

            def align_scores(c, it, l):
                pe.wait_ge(batch_in[c], it * 48 + 48)
                pe.wait_ge(att_rd[c], nth(it, 0, 0, ST))
                for s in range(ST):
                    for k in range(DT):
                        mm = pe.matmul(ps[c][:, BANK_AL_SCORES, s * P:s * P + T_CTX], xt[c][:, k, s * P:(s + 1) * P],
                                       ct[c][:, k, 0:T_CTX], start=k == 0, stop=k == DT - 1)
                mm.then_inc(al_sc_mm[c], 1)
                pe.wait_ge(ct_split[c], 2 * it + 2)
                for k in range(DT):
                    mm = three(ps[c][0:T_CTX, BANK_AL_CW, 0:D], ct_hi[c][:, k, 0:T_CTX], ct_lo[c][:, k, 0:T_CTX],
                               wa_hi[:, DT + k, :], wa_lo[:, DT + k, :], k == 0, k == DT - 1)
                mm.then_inc(al_cw_mm[c], 1)

            def align_turn(c, it, l):
                pe.wait_ge(al_p_rd[c], it + 1)
                for s in range(ST):
                    mm = pe.transpose(ps[c][0:T_CTX, BANK_AL_SCORES, s * P:(s + 1) * P], align_p[c][:, s, :], ident[:])
                mm.then_inc(al_pt_mm[c], 1)

            def align_out(c, it, l):
                pe.wait_ge(x_split[c], 2 * it + 2)
                pe.wait_ge(lnt_rd[c], nth(it, 0, 0))
                pe.wait_ge(u_rd[c], nth(it, 0, 0))
                for m in range(DT):
                    for k in range(DT):
                        three(ps[c][:, BANK_AL_X[m], 0:S], wa_hi[:, k, m * P:(m + 1) * P], wa_lo[:, k, m * P:(m + 1) * P],
                              xt_hi[c][:, k, :], xt_lo[c][:, k, :], k == 0, False)
                pe.wait_ge(al_pt_rd[c], it + 1)
                pe.wait_ge(cw_rd[c], it + 1)
                for m in range(DT):
                    pe.matmul(ps[c][:, BANK_AL_X[m], 0:S], cw[c][0:T_CTX, m * P:(m + 1) * P], align_pt[c][0:T_CTX, :],
                              start=False, stop=True).then_inc(al_x_mm[c], 1)

            def keys(c, it, l):
                pe.wait_ge(enc_rd[c], nth(it, l))
                if l == 0:
                    pe.wait_ge(cw_rd[c], it + 1)
                else:
                    pe.wait_ge(att_rd[c], nth(it, l, 0, ST))
                for s in range(ST):
                    for m in range(DT):
                        mm = pe.transpose(bank2(c, BANK_NATURAL)[:, s, m * P:(m + 1) * P], enc_t[c][:, m, s * P:(s + 1) * P], ident[:])
                mm.then_inc(nat_mm[c], 1)
                if l == 0:
                    pe.wait_ge(al_pt_rd[c], it + 1)
                    for m in range(DT):
                        for k in range(DT):
                            mm = pe.matmul(bank2(c, BANK_K)[:, m, 0:T_CTX], wk0[:, k, m * P:(m + 1) * P], ct[c][:, k, 0:T_CTX],
                                           start=k == 0, stop=k == DT - 1)
                else:
                    pe.wait_ge(enchi_rd[c], nth(it, l))
                    pe.wait_ge(enclo_rd[c], nth(it, l))
                    mm = project(bank2(c, BANK_K), l, 1, enc_hi[c], enc_lo[c])
                mm.then_inc(k_mm[c], 1)

            def queries(c, it, l):
                pe.wait_ge(enchi_rd[c], nth(it, l))
                pe.wait_ge(enclo_rd[c], nth(it, l))
                if l == 0:
                    pe.wait_ge(th_rd[c], it + 1)
                else:
                    pe.wait_ge(lnt_rd[c], nth(it, l, 0))
                    pe.wait_ge(u_rd[c], nth(it, l, 0))
                project(bank2(c, BANK_Q), l, 0, enc_hi[c], enc_lo[c], (0,))
                pe.wait_ge(keepk_rd[c], 2 * nth(it, l))
                for b, (t, n) in enumerate(key_blocks(l)):
                    mm = pe.matmul(ps[c][:, BANK_ROW, t:t + n], keep_bf[c][0:n, b:b + 1].broadcast_to([n, P]), ident_bf[0:n, 0:n],
                                   start=True, stop=True)
                mm.then_inc(row_mm[c], 1)
                project(bank2(c, BANK_Q), l, 0, enc_hi[c], enc_lo[c], (1,)).then_inc(q_mm[c], 1)

            def values(c, it, l):
                pe.wait_ge(p_rd[c], nth(it, l, 2, 2 * HEADS))
                a_hi, a_lo = (ct_hi, ct_lo) if l == 0 else (enc_hi, enc_lo)
                for b, (t, n) in enumerate(key_blocks(l)):
                    out = bank2(c, BANK_V)[0:n, b, :]
                    for k in range(DT):
                        three(out, a_hi[c][:, k, t:t + n], a_lo[c][:, k, t:t + n], w_hi[:, l, 2, k, :], w_lo[:, l, 2, k, :],
                              k == 0, False)
                    mm = pe.matmul(out, ones_r[:, 0:n], bv_split[:, l, :], start=False, stop=True)
                mm.then_inc(v_mm[c], 1)

            def scores(c, it, l):
                n = T_CTX if l == 0 else S
                pe.wait_ge(q_rd[c], nth(it, l))
                pe.wait_ge(k_rd[c], nth(it, l))
                for s in range(ST):
                    if s == 1:
                        pe.wait_ge(nat_rd[c], nth(it, l))
                        pe.wait_ge(row_rd[c], nth(it, l))
                    for j in ISSUE_ORDER:
                        h = HEAD_OF_SLOT[j]
                        rows = slice(DH * (h % 2), DH * (h % 2) + DH)
                        mm = pe.matmul(bank2(c, 2 * s + j // 2)[:, j % 2, 0:n], qt[c][rows, h // 2, s * P:(s + 1) * P],
                                       kt[c][rows, h // 2, 0:n], start=True, stop=True)
                    mm.then_inc(sc_mm[c], 1)

            def turn(c, it, l, slots):
                for j in slots:
                    pe.wait_ge(p_rd[c], nth(it, l, HEADS + j + 1, 2 * HEADS))
                    if BANK_OF_TURN[j] == BANK_V:
                        pe.wait_ge(v_rd[c], nth(it, l))
                    for b, (t, n) in enumerate(key_blocks(l)):
                        for s in range(ST):
                            mm = pe.transpose(bank2(c, BANK_OF_TURN[j])[0:n, b, s * P:(s + 1) * P], prob[c][:, s, j, t:t + n], ident[:])
                    mm.then_inc(pt_mm[c], 1)

            def turn_a(c, it, l):
                turn(c, it, l, (0, 1))

            def turn_b(c, it, l):
                turn(c, it, l, (2, 3))

            def mix(c, it, l):
                pe.wait_ge(vcol_rd[c], nth(it, l))
                pe.wait_ge(v_rd[c], nth(it, l))
                blocks = key_blocks(l)
                for s in range(ST):
                    for j in range(HEADS):
                        h = HEAD_OF_SLOT[j]
                        if s == 0:
                            pe.wait_ge((pta_rd, ptd_rd)[j % 2][c], nth(it, l, j // 2 + 1, 2))
                        for b, (t, n) in enumerate(blocks):
                            mm = pe.matmul(ps[c][:, BANK_MIX + s, h * VH:(h + 1) * VH], prob_t[c][0:n, j, b, s * P:(s + 1) * P],
                                           v[c][0:n, b, h, :], start=b == 0, stop=b == len(blocks) - 1)
                    mm.then_inc(av_mm[c], 1)

            def norm(c, it, l):
                for s in range(ST):
                    pe.wait_ge(z_rd[c], nth(it, l, s + 1, ST))
                    for m in range(DT):
                        mm = pe.transpose(bank2(c, BANK_ZT)[:, m, s * P:(s + 1) * P], z[c][:, s, m * P:(m + 1) * P], ident[:])
                mm.then_inc(zt_mm[c], 1)

            def feed(c, it, l):
                pe.wait_ge(lnhi_rd[c], nth(it, l))
                pe.wait_ge(lnlo_rd[c], nth(it, l))
                project(bank2(c, BANK_FF), l, 3, ln_hi[c], ln_lo[c]).then_inc(ff_mm[c], 1)

            steps = dict(align_scores=align_scores, align_turn=align_turn, align_out=align_out,
                         keys=keys, queries=queries, scores=scores, values=values, turn_a=turn_a, turn_b=turn_b, mix=mix,
                         norm=norm, feed=feed)
            pe.wait_ge(const_in, 64)
            pe.wait_ge(const_rd, 4)
            pe.wait_ge(bias_rd, 3)
            pe.wait_ge(w_split, 2 * (1 + 2 * LAYERS))
            pe.wait_ge(wk0_in, 16)
            run_steps(pe.Fori, lambda name, c, it, l: steps[name](c, it, l) if name in steps else None)

        @block.scalar
        def _(act):
            def col(kind, l, m):
                return cols[:, kind, l, m:m + 1]

            def align_scores(c, it, l):
                act.wait_ge(al_max_rd[c], it + 1)
                for s in range(ST):
                    act.activation(align_e[c][:, s, :], ps[c][:, BANK_AL_SCORES, s * P:s * P + T_CTX], ACT.Exp,
                                   bias=align_nmax[c][:, s:s + 1], accum_out=align_sum[c][:, s:s + 1]).then_inc(al_e_rd[c], 1)
                act.wait_ge(al_cw_mm[c], it + 1)
                act.activation(cw[c][0:T_CTX, :], ps[c][0:T_CTX, BANK_AL_CW, 0:D], ACT.Copy).then_inc(cw_rd[c], 1)

            def align_out(c, it, l):
                for m in range(DT):
                    act.wait_ge(al_x_mm[c], DT * it + m + 1)
                    ins = act.activation(th[c][:, m, :], ps[c][:, BANK_AL_X[m], 0:S], ACT.Tanh, bias=col(COL_BT, 0, m))
                ins.then_inc(th_rd[c], 1)
                enc_high(c, it, 0)

            def keys(c, it, l):
                act.wait_ge(nat_mm[c], nth(it, l))
                for s in range(ST):
                    ins = act.activation(enc_n[c][:, s, :], bank2(c, BANK_NATURAL)[:, s, :], ACT.Copy, accum_out=enc_sum[c][:, s:s + 1])
                ins.then_inc(nat_rd[c], 1)
                n = T_CTX if l == 0 else S
                act.wait_ge(k_mm[c], nth(it, l))
                act.wait_ge(k_rd[c], nth(it, l, 0))
                for m in range(DT):
                    ins = act.activation(kt_raw[c][:, m, 0:n], bank2(c, BANK_K)[:, m, 0:n], ACT.Relu, bias=col(COL_BK, l, m))
                ins.then_inc(kraw_rd[c], 1)

            def queries(c, it, l):
                n = T_CTX if l == 0 else S
                act.wait_ge(row_mm[c], nth(it, l))
                act.wait_ge(k_rd[c], nth(it, l, 0))
                act.activation(keep_row[c][:, 0:n], ps[c][:, BANK_ROW, 0:n], ACT.Copy, accum_out=any_keep[c][:]).then_inc(row_rd[c], 1)
                act.wait_ge(q_mm[c], nth(it, l))
                for m in range(DT):
                    ins = act.activation(qt[c][:, m, :], bank2(c, BANK_Q)[:, m, :], ACT.Relu, bias=bq_scaled[:, l, m:m + 1],
                                         scale=float(DH) ** -0.5)
                ins.then_inc(q_rd[c], 1)

            def scores(c, it, l):
                n = T_CTX if l == 0 else S
                for s in range(ST):
                    for j in range(HEADS):
                        if j % 2 == 0:
                            act.wait_ge(max_rd[c], nth(it, l, 2 * s + j // 2 + 1, 2 * ST))
                        act.activation(prob[c][:, s, j, 0:n], bank2(c, 2 * s + j // 2)[:, j % 2, 0:n], ACT.Exp,
                                       bias=nmax[c][:, s, j:j + 1]).then_inc(p_rd[c], 1)

            def turn(c, it, l, j):
                n, nb = (T_CTX, 1) if l == 0 else (P, ST)
                act.wait_ge(pt_mm[c], nth(it, l, j + 1, HEADS))
                act.activation(prob_t[c][0:n, j, 0:nb, :], bank2(c, BANK_OF_TURN[j])[0:n, 0:nb, :], ACT.Copy).then_inc(pta_rd[c], 1)

            def turn_a(c, it, l):
                turn(c, it, l, 0)

            def turn_b(c, it, l):
                turn(c, it, l, 2)

            def norm(c, it, l):
                act.wait_ge(zt_mm[c], nth(it, l))
                for m in range(DT):
                    ins = act.activation(ln_t[c][:, m, :], bank2(c, BANK_ZT)[:, m, :], ACT.Identity, bias=col(COL_BETA, l, m),
                                         scale=col(COL_GAMMA, l, m))
                ins.then_inc(lnt_rd[c], 1)

            def enc_high(c, it, l):
                act.wait_ge(enc_rd[c], nth(it, l))
                act.activation(enc_hi[c][:], enc_t[c][:], ACT.Copy).then_inc(enchi_rd[c], 1)

            def encode(c, it, l):
                if l < LAYERS - 1:
                    enc_high(c, it, l + 1)

            def align_split(c, it, l):
                act.wait_ge(batch_in[c], it * 48 + 48)
                act.wait_ge(al_x_mm[c], DT * it)
                act.activation(xt_hi[c][:], xt[c][:], ACT.Copy).then_inc(x_split[c], 1)

            def leak(c, it, l):
                act.wait_ge(ff_mm[c], nth(it, l))
                for m in range(DT):
                    ins = act.activation(ff[c][:, m, :], bank2(c, BANK_FF)[:, m, :], ACT.Identity, bias=col(COL_BFF, l, m))
                ins.then_inc(u_rd[c], 1)

            steps = dict(align_split=align_split, align_scores=align_scores, align_out=align_out, keys=keys, queries=queries,
                         scores=scores, turn_a=turn_a, turn_b=turn_b, norm=norm, leak=leak, encode=encode)
            act.wait_ge(const_in, 64)
            act.wait_ge(const_rd, 4)
            run_steps(act.Fori, lambda name, c, it, l: steps[name](c, it, l) if name in steps else None)

        @block.gpsimd
        def _(pool):
            def mix(c, it, l):
                pool.wait_ge(var_rd[c], nth(it, l, 2, ST))
                pool.tensor_tensor(std[c][:], var[c][:], half[:], ALU.pow).then_inc(std_rd[c], 1)

            def align_split(c, it, l):
                pool.wait_ge(x_split[c], 2 * it + 1)
                pool.tensor_tensor(xt_lo[c][:], xt[c][:], xt_hi[c][:].bitcast(F32), ALU.subtract).then_inc(x_split[c], 1)

            def queries(c, it, l):
                n = T_CTX if l == 0 else S
                pool.wait_ge(kraw_rd[c], nth(it, l))
                pool.wait_ge(row_rd[c], nth(it, l))
                pool.tensor_tensor(kt[c][:, :, 0:n], kt_raw[c][:, :, 0:n],
                                   keep_row[c][:, 0:n].unsqueeze(1).broadcast_to([P, DT, n]), ALU.mult).then_inc(k_rd[c], 1)

            def enc_low(c, it, l):
                pool.wait_ge(enchi_rd[c], nth(it, l))
                pool.tensor_tensor(enc_lo[c][:], enc_t[c][:], enc_hi[c][:].bitcast(F32), ALU.subtract).then_inc(enclo_rd[c], 1)

            def encode(c, it, l):
                last = l == LAYERS - 1
                pool.wait_ge(ffl_rd[c], nth(it, l))
                pool.tensor_tensor(enc_t[c][:], ffl[c][:], ln_t[c][:], ALU.add).then_inc(final_rd[c] if last else enc_rd[c], 1)
                if not last:
                    enc_low(c, it, l + 1)

            def align_out(c, it, l):
                pool.wait_ge(th_rd[c], it + 1)
                pool.wait_ge(out_sent[c], 16 * it)
                pool.tensor_tensor(enc_t[c][:], th[c][:], xt[c][:], ALU.add).then_inc(enc_rd[c], 1)
                enc_low(c, it, 0)

            pool.wait_ge(const_rd, 4)
            steps = dict(mix=mix, queries=queries, encode=encode, align_split=align_split, align_out=align_out)
            run_steps(pool.Fori, lambda name, c, it, l: steps[name](c, it, l) if name in steps else None)

        @block.vector
        def _(dve):
            dve.memset(ones_f[:], 1.0).then_inc(bias_rd, 1)
            dve.memset(half[:], 0.5).then_inc(const_rd, 1)
            for c in CHAINS:
                dve.memset(ct_hi[c][:].bitcast(F32), 0.0).then_inc(pad_rd, 1)
                dve.memset(ct_lo[c][:].bitcast(F32), 0.0).then_inc(pad_rd, 1)
            dve.memset(bv_split[:].bitcast(F32), 0.0).then_inc(pad_rd, 1)
            dve.wait_ge(const_in, 64)
            dve.tensor_copy(ident_bf[:], ident[:]).then_inc(const_rd, 1)
            dve.tensor_scalar(bq_scaled[:], cols[:, COL_BQ], float(DH) ** -0.5, None, ALU.mult).then_inc(const_rd, 1)
            dve.wait_ge(bias_rd, 1)
            dve.tensor_copy(ones_r[:], ones_f[:]).then_inc(const_rd, 1)
            dve.tensor_copy(bv_hi[32:33], bv[32:33]).then_inc(pad_rd, 1)
            dve.wait_ge(pad_rd, 6)
            dve.tensor_copy(bv_split[0:1], bv[0:1]).then_inc(bias_rd, 1)
            dve.tensor_tensor(bv_split[32:33], bv[32:33], bv_hi[32:33].bitcast(F32), ALU.subtract).then_inc(bias_rd, 1)
            dests = [(wa_hi[:], wa_lo[:])]
            for l in range(LAYERS):
                for pair in range(2):
                    dests.append(tuple(w[:, l, 2 * pair:2 * pair + 2].rearrange("p w k n -> p (w k) n") for w in (w_hi, w_lo)))
            for n, (hi, lo) in enumerate(dests):
                dve.wait_ge(w_in[n % 2], 16 * (n // 2 + 1))
                dve.tensor_copy(hi, stage_w[:, n % 2]).then_inc(w_split, 1)
                dve.wait_ge(w_split, 2 * n + 1)
                dve.tensor_tensor(lo, stage_w[:, n % 2], hi.bitcast(F32), ALU.subtract).then_inc(w_split, 1)

            def align_split(c, it, l):
                dve.wait_ge(batch_in[c], it * 48 + 48)
                dve.wait_ge(pad_rd, 6)
                dve.wait_ge(v_mm[c], nth(it, 0, 0))
                dve.tensor_copy(ct_hi[c][:, :, 0:T_CTX], ct[c][:, :, 0:T_CTX]).then_inc(ct_split[c], 1)
                dve.tensor_reduce(c_sum[c][0:T_CTX], cn[c][0:T_CTX, :], AX.X, ALU.add).then_inc(csum_rd[c], 1)
                dve.wait_ge(ct_split[c], 2 * it + 1)
                dve.tensor_tensor(ct_lo[c][:, :, 0:T_CTX], ct[c][:, :, 0:T_CTX], ct_hi[c][:, :, 0:T_CTX].bitcast(F32),
                                  ALU.subtract).then_inc(ct_split[c], 1)
                dve.wait_ge(csum_rd[c], it + 1)
                dve.tensor_scalar(c_keep[c][0:T_CTX], c_sum[c][0:T_CTX], 0.0, None, ALU.not_equal).then_inc(ckeep_rd[c], 1)

            def align_scores(c, it, l):
                dve.wait_ge(al_sc_mm[c], it + 1)
                dve.tensor_reduce(align_nmax[c][:], ps[c][:, BANK_AL_SCORES, 0:S].rearrange("p (s t) -> p s t", s=ST)[:, :, 0:T_CTX], AX.X,
                                  ALU.max, negate=True).then_inc(al_max_rd[c], 1)
                dve.wait_ge(al_e_rd[c], 2 * it + 2)
                dve.reciprocal(align_rsum[c][:], align_sum[c][:]).then_inc(al_rs_rd[c], 1)
                dve.wait_ge(al_rs_rd[c], it + 1)
                dve.tensor_tensor(align_p[c][:], align_e[c][:], align_rsum[c][:].unsqueeze(2).broadcast_to([P, ST, T_CTX]),
                                  ALU.mult).then_inc(al_p_rd[c], 1)

            def align_turn(c, it, l):
                dve.wait_ge(al_pt_mm[c], it + 1)
                dve.tensor_copy(align_pt[c][0:T_CTX, :], ps[c][0:T_CTX, BANK_AL_SCORES, 0:S]).then_inc(al_pt_rd[c], 1)

            def keys(c, it, l):
                dve.wait_ge(nat_rd[c], nth(it, l))
                dve.tensor_scalar(keep_q[c][:], enc_sum[c][:], 0.0, None, ALU.not_equal).then_inc(keepq_rd[c], 1)
                n, nb = (T_CTX, 1) if l == 0 else (P, ST)
                if l == 0:
                    src = c_keep[c][0:n, 0:1]
                else:
                    dve.wait_ge(keepq_rd[c], nth(it, l))
                    src = keep_q[c][:]
                dve.tensor_copy(keep_k[c][0:n, 0:nb], src).then_inc(keepk_rd[c], 1)
                dve.tensor_copy(keep_bf[c][0:n, 0:nb], src).then_inc(keepk_rd[c], 1)

            def queries(c, it, l):
                n, nb, keys = (T_CTX, 1, T_CTX) if l == 0 else (P, ST, S)
                dve.wait_ge(row_rd[c], nth(it, l))
                dve.tensor_scalar(none_keep[c][:], any_keep[c][:], 0.0, None, ALU.is_equal).then_inc(none_rd[c], 1)
                dve.wait_ge(none_rd[c], nth(it, l))
                dve.tensor_scalar(keep_v[c][0:n, 0:nb], keep_k[c][0:n, 0:nb], none_keep[c][0:n, 0:1], None,
                                  ALU.max).then_inc(keepv_rd[c], 1)
                dve.wait_ge(keepv_rd[c], nth(it, l))
                dve.tensor_copy(v[c][0:n, 0:nb, :, DH], keep_v[c][0:n, 0:nb].unsqueeze(2).broadcast_to([n, nb, HEADS])
                                ).then_inc(vcol_rd[c], 1)

            def scores(c, it, l):
                n = T_CTX if l == 0 else S
                for s in range(ST):
                    dve.wait_ge(sc_mm[c], nth(it, l, s + 1, ST))
                    for b in range(2):
                        dve.tensor_reduce(nmax[c][:, s, 2 * b:2 * b + 2], bank2(c, 2 * s + b)[:, :, 0:n],
                                          AX.X, ALU.max, negate=True).then_inc(max_rd[c], 1)

            def values(c, it, l):
                dve.wait_ge(v_mm[c], nth(it, l))
                for b, (t, k) in enumerate(key_blocks(l)):
                    ins = dve.tensor_scalar(v[c][0:k, b, :, 0:DH], bank2(c, BANK_V)[0:k, b, :].rearrange("p (h d) -> p h d", h=HEADS),
                                            keep_v[c][0:k, b:b + 1], 0.0, ALU.mult, ALU.max)
                ins.then_inc(v_rd[c], 1)

            def turn(c, it, l, j):
                n, nb = (T_CTX, 1) if l == 0 else (P, ST)
                dve.wait_ge(pt_mm[c], nth(it, l, j + 1, HEADS))
                dve.tensor_copy(prob_t[c][0:n, j, 0:nb, :], bank2(c, BANK_OF_TURN[j])[0:n, 0:nb, :]).then_inc(ptd_rd[c], 1)

            def turn_a(c, it, l):
                turn(c, it, l, 1)

            def turn_b(c, it, l):
                turn(c, it, l, 3)

            def mix(c, it, l):
                att_h = att[c][:].rearrange("p s (h d) -> p s h d", h=HEADS)

                def scale_mix(s):
                    o = ps[c][:, BANK_MIX + s, 0:HEADS * VH].rearrange("p (h d) -> p h d", h=HEADS)
                    dve.wait_ge(av_mm[c], nth(it, l, s + 1, ST))
                    dve.reciprocal(rsum[c][:, s], o[:, :, DH]).then_inc(rsum_rd[c], 1)
                    dve.wait_ge(rsum_rd[c], nth(it, l, s + 1, ST))
                    dve.tensor_scalar(rscale[c][:, s], rsum[c][:, s], keep_q[c][:, s:s + 1], None, ALU.mult).then_inc(rscale_rd[c], 1)
                    dve.wait_ge(rscale_rd[c], nth(it, l, s + 1, ST))
                    dve.tensor_tensor(att_h[:, s], o[:, :, 0:DH], rscale[c][:, s].unsqueeze(2).broadcast_to([P, HEADS, DH]),
                                      ALU.mult).then_inc(att_rd[c], 1)

                def add_input(s):
                    dve.wait_ge(att_rd[c], nth(it, l, s + 1, ST))
                    dve.tensor_tensor(res[c][:, s, :], att[c][:, s, :], enc_n[c][:, s, :], ALU.add).then_inc(res_rd[c], 1)

                def stats(s):
                    dve.wait_ge(res_rd[c], nth(it, l, s + 1, ST))
                    dve.bn_stats(bn[c][:, s, :], res[c][:, s, :]).then_inc(bn_rd[c], 1)

                def variance(s):
                    dve.wait_ge(mv_rd[c], nth(it, l, s + 1, ST))
                    dve.tensor_scalar(var[c][:, s:s + 1], mv[c][:, s, 1:2], D / (D - 1.0), None, ALU.mult).then_inc(var_rd[c], 1)

                scale_mix(0)
                add_input(0)
                stats(0)
                scale_mix(1)
                dve.wait_ge(bn_rd[c], nth(it, l, 1, ST))
                add_input(1)
                dve.bn_aggr(mv[c][:, 0, :], bn[c][:, 0, :]).then_inc(mv_rd[c], 1)
                stats(1)
                dve.wait_ge(bn_rd[c], nth(it, l, 2, ST))
                variance(0)
                dve.bn_aggr(mv[c][:, 1, :], bn[c][:, 1, :]).then_inc(mv_rd[c], 1)
                variance(1)

            def center(c, it, l):
                dve.wait_ge(std_rd[c], nth(it, l))
                dve.tensor_scalar(std_eps[c][:], std[c][:], EPS, None, ALU.add).then_inc(stde_rd[c], 1)
                dve.wait_ge(stde_rd[c], nth(it, l))
                dve.reciprocal(rstd[c][:], std_eps[c][:]).then_inc(rstd_rd[c], 1)
                dve.wait_ge(rstd_rd[c], nth(it, l))
                for s in range(ST):
                    dve.tensor_scalar(z[c][:, s, :], res[c][:, s, :], mv[c][:, s, 0:1], rstd[c][:, s:s + 1], ALU.subtract,
                                      ALU.mult).then_inc(z_rd[c], 1)

            def norm(c, it, l):
                dve.wait_ge(lnt_rd[c], nth(it, l))
                dve.tensor_copy(ln_hi[c][:], ln_t[c][:]).then_inc(lnhi_rd[c], 1)
                dve.wait_ge(lnhi_rd[c], nth(it, l))
                dve.tensor_tensor(ln_lo[c][:], ln_t[c][:], ln_hi[c][:].bitcast(F32), ALU.subtract).then_inc(lnlo_rd[c], 1)

            def leak(c, it, l):
                dve.wait_ge(u_rd[c], nth(it, l))
                dve.scalar_tensor_tensor(ffl[c][:], ff[c][:], LEAK, ff[c][:], ALU.mult, ALU.max).then_inc(ffl_rd[c], 1)

            steps = dict(align_split=align_split, align_scores=align_scores, align_turn=align_turn,
                         keys=keys, queries=queries, scores=scores, values=values, turn_a=turn_a, turn_b=turn_b, mix=mix,
                         center=center, norm=norm, leak=leak)
            run_steps(dve.Fori, lambda name, c, it, l: steps[name](c, it, l) if name in steps else None)


def columns_of(vectors):
    n, layers, d = vectors.shape
    return np.ascontiguousarray(vectors.reshape(n, layers, d // P, P).transpose(3, 0, 1, 2))


def kernel(**inputs):
    import concourse.bacc as bacc
    from concourse.bass_utils import run_bass_kernel_spmd

    a = {k: np.asarray(x) for k, x in inputs.items()}
    bt = a["L0_xattn_trans_b"]
    arrays = {
        "x_t": np.ascontiguousarray(a["x"].transpose(0, 2, 1)),
        "ctx_t": np.ascontiguousarray(a["ctx_1024"].transpose(0, 2, 1)),
        "ctx_n": np.ascontiguousarray(a["ctx_1024"]),
        "w_align": np.ascontiguousarray(a["L0_xattn_trans_W"]),
        "w_qkvf": np.ascontiguousarray(np.stack([a["L1_xattn_Wq"], a["L1_xattn_Wk"], a["L1_xattn_Wv"], a["L1_xattn_Wff"]], 1)),
        "columns": columns_of(np.stack([a["L1_xattn_bq"], a["L1_xattn_bk"], a["L1_xattn_gamma"], a["L1_xattn_beta"],
                                        a["L1_xattn_bff"], np.stack([bt] * LAYERS)])),
        "bv_row": np.ascontiguousarray(a["L1_xattn_bv"][None]),
        "identity": np.eye(P, dtype=np.float32),
    }
    nc = bacc.Bacc("TRN2", target_bir_lowering=False, num_devices=1)
    aps = [nc.dram_tensor(f"in_{n}", x.shape, mybir.dt.from_np(x.dtype), kind="ExternalInput").ap() for n, x in arrays.items()]
    b, s, d = a["x"].shape
    out = nc.dram_tensor("out_t", (b, d, s), F32, kind="ExternalOutput").ap()
    build_program(nc, *aps, out)
    r = run_bass_kernel_spmd(nc, [{f"in_{n}": x for n, x in arrays.items()}], core_ids=[0])
    return np.ascontiguousarray(r.results[0]["out_t"].transpose(0, 2, 1))
```

```python
from contextlib import ExitStack

import numpy as np

import concourse.bass as bass
from concourse import mybir

ALU = mybir.AluOpType
ACT = mybir.ActivationFunctionType
AX = mybir.AxisListType
F32 = mybir.dt.float32
F32R = mybir.dt.float32r
BF16 = mybir.dt.bfloat16

P = 128
LAYERS = 3
HEADS = 4
EPS = 1e-8
LEAK = 0.2
COL_BQ, COL_BK, COL_GAMMA, COL_BETA, COL_BFF, COL_BT = 0, 1, 2, 3, 4, 5
HEAD_OF_SLOT = [0, 2, 1, 3]
ISSUE_ORDER = [0, 2, 1, 3]


def build_program(nc, x_t, ctx_t, ctx_n, w_align, w_qkvf, columns, bv_row, identity, out_t):
    batches, D, S = x_t.shape
    T_CTX = ctx_n.shape[1]
    DT = D // P
    ST = S // P
    DH = D // HEADS
    ROUNDS = batches // 2
    CTX_PAD = T_CTX + T_CTX % 2
    VH = DH + 1
    assert D == 2 * P and S == 2 * P and DH == 64 and batches % 2 == 0 and T_CTX < P
    CHAINS = range(2)

    with ExitStack() as ctx:
        def sb(name, shape, dt=F32):
            return ctx.enter_context(nc.sbuf_tensor(name, shape, dt))

        def sb2(name, shape, dt=F32):
            return [sb(f"{name}_{c}", shape, dt) for c in "ab"]

        def sem(name):
            return ctx.enter_context(nc.semaphore(name))

        def sem2(name):
            return [sem(f"{name}_{c}") for c in "ab"]

        stage_w = sb("stage_w", [P, 2, 4, D])
        wa_hi = sb("wa_hi", [P, 2 * DT, D], F32R)
        wa_lo = sb("wa_lo", [P, 2 * DT, D], F32R)
        w_hi = sb("w_hi", [P, LAYERS, 4, DT, D], F32R)
        w_lo = sb("w_lo", [P, LAYERS, 4, DT, D], F32R)
        wk0 = sb("wk0", [P, DT, D])
        cols = sb("cols", [P, 6, LAYERS, DT])
        bq_scaled = sb("bq_scaled", [P, LAYERS, DT])
        ident = sb("ident", [P, P])
        ident_bf = sb("ident_bf", [P, P], BF16)
        ones_f = sb("ones_f", [P, P])
        ones_r = sb("ones_r", [P, P], F32R)
        half = sb("half", [P, ST])
        bv = sb("bv", [P, LAYERS, D])
        bv_hi = sb("bv_hi", [P, LAYERS, D], F32R)
        bv_split = sb("bv_split", [P, LAYERS, D], F32R)

        xt = sb2("xt", [P, DT, S])
        xt_hi = sb2("xt_hi", [P, DT, S], F32R)
        xt_lo = sb2("xt_lo", [P, DT, S], F32R)
        ct = sb2("ct", [P, DT, CTX_PAD])
        ct_hi = sb2("ct_hi", [P, DT, CTX_PAD], F32R)
        ct_lo = sb2("ct_lo", [P, DT, CTX_PAD], F32R)
        cn = sb2("cn", [P, D])
        c_sum = sb2("c_sum", [P, 1])
        align_nmax = sb2("align_nmax", [P, ST])
        align_sum = sb2("align_sum", [P, ST])
        align_rsum = sb2("align_rsum", [P, ST])
        align_e = sb2("align_e", [P, ST, T_CTX])
        align_p = sb2("align_p", [P, ST, T_CTX])
        align_pt = sb2("align_pt", [P, S])
        cw = sb2("cw", [P, D])
        th = sb2("th", [P, DT, S])
        enc_t = sb2("enc_t", [P, DT, S])
        enc_hi = sb2("enc_hi", [P, DT, S], F32R)
        enc_lo = sb2("enc_lo", [P, DT, S], F32R)
        final = sb2("final", [P, DT, S])
        enc_n = sb2("enc_n", [P, ST, D])
        enc_sum = sb2("enc_sum", [P, ST])
        keep_q = sb2("keep_q", [P, ST])
        keep_k = sb2("keep_k", [P, ST])
        keep_bf = sb2("keep_bf", [P, ST], BF16)
        keep_row = sb2("keep_row", [P, S])
        any_keep = sb2("any_keep", [P, 1])
        none_keep = sb2("none_keep", [P, 1])
        keep_v = sb2("keep_v", [P, ST])
        qt = sb2("qt", [P, DT, S])
        kt_raw = sb2("kt_raw", [P, DT, S])
        kt = sb2("kt", [P, DT, S])
        v = sb2("v", [P, ST, HEADS, VH])
        nmax = sb2("nmax", [P, ST, HEADS])
        prob = sb2("prob", [P, ST, HEADS, S])
        prob_t = sb2("prob_t", [P, HEADS, ST, S])
        rsum = sb2("rsum", [P, ST, HEADS])
        rscale = sb2("rscale", [P, ST, HEADS])
        att = sb2("att", [P, ST, D])
        res = sb2("res", [P, ST, D])
        bn = sb2("bn", [P, ST, 6])
        mv = sb2("mv", [P, ST, 2])
        var = sb2("var", [P, ST])
        std = sb2("std", [P, ST])
        std_eps = sb2("std_eps", [P, ST])
        rstd = sb2("rstd", [P, ST])
        z = sb2("z", [P, ST, D])
        ln_t = sb2("ln_t", [P, DT, S])
        ln_hi = sb2("ln_hi", [P, DT, S], F32R)
        ln_lo = sb2("ln_lo", [P, DT, S], F32R)
        ff = sb2("ff", [P, DT, S])

        ps = [ctx.enter_context(nc.psum_tensor(f"ps_{c}", [P, 4, 512], F32)) for c in "ab"]

        const_in = sem("const_in")
        w_in = [sem(f"w_in_{n}") for n in range(2)]
        wk0_in = sem("wk0_in")
        w_split = sem("w_split")
        const_rd = sem("const_rd")
        bias_rd = sem("bias_rd")
        pad_rd = sem("pad_rd")
        batch_in = sem2("batch_in")
        out_sent = sem2("out_sent")
        al_sc_mm, al_pt_mm, al_x_mm = (sem2(s) for s in ("al_sc_mm", "al_pt_mm", "al_x_mm"))
        nat_mm, q_mm, k_mm, row_mm = (sem2(s) for s in ("nat_mm", "q_mm", "k_mm", "row_mm"))
        va_mm, vb_mm = (sem2(s) for s in ("va_mm", "vb_mm"))
        sc_mm, pt_mm, av_mm, zt_mm, ff_mm = (sem2(s) for s in ("sc_mm", "pt_mm", "av_mm", "zt_mm", "ff_mm"))
        al_e_rd, cw_rd, th_rd = (sem2(s) for s in ("al_e_rd", "cw_rd", "th_rd"))
        nat_rd, q_rd, kraw_rd, p_rd = (sem2(s) for s in ("nat_rd", "q_rd", "kraw_rd", "p_rd"))
        pta_rd, lnt_rd, u_rd = (sem2(s) for s in ("pta_rd", "lnt_rd", "u_rd"))
        x_split, ct_split, csum_rd = (sem2(s) for s in ("x_split", "ct_split", "csum_rd"))
        al_max_rd, al_rs_rd, al_p_rd, al_pt_rd = (sem2(s) for s in ("al_max_rd", "al_rs_rd", "al_p_rd", "al_pt_rd"))
        keepq_rd, keepk_rd, row_rd, none_rd = (sem2(s) for s in ("keepq_rd", "keepk_rd", "row_rd", "none_rd"))
        keepv_rd, vcol_rd, max_rd, ptd_rd = (sem2(s) for s in ("keepv_rd", "vcol_rd", "max_rd", "ptd_rd"))
        rsum_rd, rscale_rd, att_rd, res_rd, bn_rd = (sem2(s) for s in ("rsum_rd", "rscale_rd", "att_rd", "res_rd", "bn_rd"))
        va_rd, vb_rd = (sem2(s) for s in ("va_rd", "vb_rd"))
        mv_rd, var_rd, stde_rd, rstd_rd, z_rd = (sem2(s) for s in ("mv_rd", "var_rd", "stde_rd", "rstd_rd", "z_rd"))
        lnhi_rd, ffl_rd, enc_rd, enchi_rd, final_rd = (sem2(s) for s in ("lnhi_rd", "ffl_rd", "enc_rd", "enchi_rd", "final_rd"))
        lnlo_rd, enclo_rd = (sem2(s) for s in ("lnlo_rd", "enclo_rd"))
        k_rd = [sem2(f"k{m}_rd") for m in range(DT)]
        std_rd = sem2("std_rd")

        def nth(it, l, j=1, per=1):
            return it * (LAYERS * per) + (l * per + j)

        def first_batch(it):
            return isinstance(it, int) and it == 0

        def last_batch(it):
            return isinstance(it, int) and it == ROUNDS - 1

        def nth_vb(it, l):
            return it * (LAYERS - 1) + l

        def key_blocks(l):
            return [(0, T_CTX)] if l == 0 else [(s * P, P) for s in range(ST)]

        def bank2(c, b):
            return ps[c][:, b].rearrange("p (m s) -> p m s", m=2)

        BANK_Q, BANK_NATURAL, BANK_ROW = 0, 2, 3
        BANK_K = [[1, 1]] + [[1, 2]] * (LAYERS - 1)
        BANK_VA, BANK_VB, BANK_ZT, BANK_FF = 3, 0, 0, 3
        BANK_OF_TURN = [1, 2, 0, 3]
        BANK_MIX = 1
        BANK_AL_SCORES = 1
        BANK_AL_X = [2, 0]
        AL_CW = slice(D, 2 * D)

        def run_steps(fori, do):
            A, B = 0, 1

            def tail(c, l, it):
                late = dict(turn_b=["leak_b", "encode"]) if l < LAYERS - 1 else dict(turn_b=["leak_b"], mix=["encode"])
                return dict(first=["spread"], keys=["center"], scores_a=["norm", "norm_parts"], values_b=["feed"],
                            turn_a=["leak_a"], **late), c, l, it

            def split(c, it):
                return dict(turn_b=["align_split"], mix=["align_split_low"]), c, 0, it

            def align_a(it):
                return dict(queries=["align_scores"], values_a=["align_probs"], scores_b=["align_turn", "align_x"],
                            values_b=["align_out"], turn_b=["align_encode"]), A, 0, it

            def align_b_attention(it):
                return dict(scores_b=["align_scores", "align_probs"], values_b=["align_turn"]), B, 0, it

            def align_b_output(it):
                return dict(scores_b=["align_x"], values_b=["align_out"], turn_b=["align_encode"]), B, 0, it

            def attention(c, l, it, *between):
                def others(name):
                    for places, c2, l2, it2 in between:
                        for other in places.get(name, []):
                            do(other, c2, it2, l2)

                for name in ["natural", "queries", "keys", "values_a", "scores_a", "scores_b", "values_b", "turn_a", "turn_b", "mix"]:
                    do(name, c, it, l)
                    if name == "natural":
                        others("first")
                    others(name)

            def alone(*groups):
                for places, c, l, it in groups:
                    for names in places.values():
                        for name in names:
                            do(name, c, it, l)

            def chain_round(it_b, it_a, first, last):
                attention(A, 0, it_a, *([] if first else [tail(B, 0, it_b)]), align_b_attention(it_a))
                if first:
                    alone(tail(A, 0, it_a))
                else:
                    attention(B, 1, it_b, tail(A, 0, it_a))
                attention(A, 1, it_a, *([] if first else [tail(B, 1, it_b)]))
                if first:
                    alone(tail(A, 1, it_a))
                else:
                    attention(B, 2, it_b, tail(A, 1, it_a))
                attention(A, 2, it_a, *([] if first else [tail(B, 2, it_b)]), align_b_output(it_a),
                          *([] if last else [split(A, it_a + 1)]))
                attention(B, 0, it_a, tail(A, 2, it_a), *([] if last else [align_a(it_a + 1), split(B, it_a + 1)]))

            alone(split(A, 0), align_a(0), split(B, 0))
            chain_round(None, 0, True, False)
            with fori(0, ROUNDS - 2) as it:
                chain_round(it, it + 1, False, False)
            chain_round(ROUNDS - 2, ROUNDS - 1, False, True)
            alone(tail(B, 0, ROUNDS - 1))
            for l in (1, 2):
                attention(B, l, ROUNDS - 1)
                alone(tail(B, l, ROUNDS - 1))

        block = ctx.enter_context(nc.Block())

        W_LOADS = 1 + LAYERS

        @block.sync
        def _(sp):
            def load(c, b):
                sp.dma_start(xt[c][:], x_t[b].rearrange("(k p) s -> p k s", p=P)).then_inc(batch_in[c], 16)
                sp.dma_start(ct[c][:, :, 0:T_CTX], ctx_t[b].rearrange("(k p) s -> p k s", p=P)).then_inc(batch_in[c], 16)
                sp.dma_start(cn[c][0:T_CTX, :], ctx_n[b]).then_inc(batch_in[c], 16)

            sp.dma_start(cols[:], columns).then_inc(const_in, 16)
            sp.dma_start(ident[:], identity).then_inc(const_in, 16)
            sp.dma_start(bv[0:1], bv_row).then_inc(const_in, 16)
            sp.dma_start(bv[32:33], bv_row).then_inc(const_in, 16)
            sp.dma_start(stage_w[:, 0], w_align.rearrange("(k p) n -> p k n", p=P)).then_inc(w_in[0], 16)
            for c in CHAINS:
                load(c, c)
            n = 1
            for l in range(LAYERS):
                for pair in range(2):
                    if n >= 2:
                        sp.wait_ge(w_split, 2 * (n - 1))
                    sp.dma_start(stage_w[:, n % 2].rearrange("p (w k) n -> p w k n", w=2),
                                 w_qkvf[l, 2 * pair:2 * pair + 2].rearrange("w (k p) n -> p w k n", p=P)).then_inc(w_in[n % 2], 16)
                    n += 1
            sp.dma_start(wk0[:], w_qkvf[0, 1].rearrange("(k p) n -> p k n", p=P)).then_inc(wk0_in, 16)

            def next_batch(c, it):
                sp.wait_ge(enc_rd[c], nth(it, 0, DT, DT))
                sp.wait_ge(k_mm[c], nth(it, 0, DT, DT))
                sp.wait_ge(va_mm[c], nth(it, 0))
                load(c, (it + 1) * 2 + c)

            def store(c, it):
                sp.wait_ge(final_rd[c], DT * it + DT)
                sp.dma_start(out_t[it * 2 + c].rearrange("(k p) s -> p k s", p=P), final[c][:]).then_inc(out_sent[c], 16)

            A, B = CHAINS
            next_batch(A, 0)
            next_batch(B, 0)
            store(A, 0)
            with sp.Fori(0, ROUNDS - 2) as it:
                next_batch(A, it + 1)
                store(B, it)
                next_batch(B, it + 1)
                store(A, it + 1)
            store(B, ROUNDS - 2)
            store(A, ROUNDS - 1)
            store(B, ROUNDS - 1)
            for c in CHAINS:
                sp.wait_ge(out_sent[c], 16 * ROUNDS)

        @block.tensor
        def _(pe):
            def three(out, a_hi, a_lo, b_hi, b_lo, first, last):
                pe.matmul(out, a_hi, b_hi, start=first, stop=False)
                pe.matmul(out, a_hi, b_lo, start=False, stop=False)
                return pe.matmul(out, a_lo, b_hi, start=False, stop=last)

            def project(out, l, w, m, hi, lo):
                for k in range(DT):
                    mm = three(out[:, m, :], w_hi[:, l, w, k, m * P:(m + 1) * P], w_lo[:, l, w, k, m * P:(m + 1) * P],
                               hi[:, k, :], lo[:, k, :], k == 0, k == DT - 1)
                return mm

            def align_scores(c, it, l):
                pe.wait_ge(batch_in[c], it * 48 + 48)
                pe.wait_ge(ct_split[c], 2 * it + 2)
                pe.wait_ge(att_rd[c], nth(it, 0, 0, ST) - (0 if c == 0 or first_batch(it) else ST * (LAYERS - 1)))
                for k in range(DT):
                    three(ps[c][0:T_CTX, BANK_AL_SCORES, AL_CW], ct_hi[c][:, k, 0:T_CTX], ct_lo[c][:, k, 0:T_CTX],
                          wa_hi[:, DT + k, :], wa_lo[:, DT + k, :], k == 0, k == DT - 1)
                for s in range(ST):
                    for k in range(DT):
                        mm = pe.matmul(ps[c][:, BANK_AL_SCORES, s * P:s * P + T_CTX], xt[c][:, k, s * P:(s + 1) * P],
                                       ct[c][:, k, 0:T_CTX], start=k == 0, stop=k == DT - 1)
                mm.then_inc(al_sc_mm[c], 1)

            def align_turn(c, it, l):
                pe.wait_ge(al_p_rd[c], it + 1)
                pe.wait_ge(cw_rd[c], it + 1)
                for s in range(ST):
                    mm = pe.transpose(ps[c][0:T_CTX, BANK_AL_SCORES, s * P:(s + 1) * P], align_p[c][:, s, :], ident[:])
                mm.then_inc(al_pt_mm[c], 1)

            def align_x(c, it, l):
                pe.wait_ge(x_split[c], 2 * it + 2)
                pe.wait_ge(att_rd[c], nth(it, 0, 0, ST))
                for m in range(DT):
                    if m == 1:
                        pe.wait_ge(lnt_rd[c], nth(it, 0, 0, DT))
                    for k in range(DT):
                        three(bank2(c, BANK_AL_X[m])[:, m, :], wa_hi[:, k, m * P:(m + 1) * P], wa_lo[:, k, m * P:(m + 1) * P],
                              xt_hi[c][:, k, :], xt_lo[c][:, k, :], k == 0, False)

            def align_out(c, it, l):
                pe.wait_ge(al_pt_rd[c], it + 1)
                for m in range(DT):
                    pe.matmul(bank2(c, BANK_AL_X[m])[:, m, :], cw[c][0:T_CTX, m * P:(m + 1) * P], align_pt[c][0:T_CTX, :],
                              start=False, stop=True).then_inc(al_x_mm[c], 1)

            def natural(c, it, l):
                pe.wait_ge(enc_rd[c], nth(it, l, DT, DT))
                if l == 0:
                    pe.wait_ge(th_rd[c], DT * it + DT)
                else:
                    pe.wait_ge(att_rd[c], nth(it, l, 0, ST))
                for s in range(ST):
                    for m in range(DT):
                        mm = pe.transpose(bank2(c, BANK_NATURAL)[:, s, m * P:(m + 1) * P], enc_t[c][:, m, s * P:(s + 1) * P], ident[:])
                mm.then_inc(nat_mm[c], 1)

            def queries(c, it, l):
                pe.wait_ge(enchi_rd[c], nth(it, l, DT, DT))
                pe.wait_ge(enclo_rd[c], nth(it, l, DT, DT))
                pe.wait_ge(lnt_rd[c], nth(it, l, 0, DT))
                for m in range(DT):
                    mm = project(bank2(c, BANK_Q), l, 0, m, enc_hi[c], enc_lo[c])
                mm.then_inc(q_mm[c], 1)

            def keys(c, it, l):
                def row():
                    pe.wait_ge(u_rd[c], nth(it, l, 0))
                    pe.wait_ge(keepk_rd[c], 2 * nth(it, l))
                    for b, (t, n) in enumerate(key_blocks(l)):
                        mm = pe.matmul(ps[c][:, BANK_ROW, t:t + n], keep_bf[c][0:n, b:b + 1].broadcast_to([n, P]), ident_bf[0:n, 0:n],
                                       start=True, stop=True)
                    mm.then_inc(row_mm[c], 1)

                if c == 0 and l == 0:
                    pe.wait_ge(al_pt_rd[c], it + 1)
                if c == 1 and l == 1 and not last_batch(it):
                    pe.wait_ge(al_pt_rd[c], it + 2)
                if l == 0:
                    row()
                    for m in range(DT):
                        for k in range(DT):
                            mm = pe.matmul(bank2(c, BANK_K[l][m])[:, m, 0:T_CTX], wk0[:, k, m * P:(m + 1) * P], ct[c][:, k, 0:T_CTX],
                                           start=k == 0, stop=k == DT - 1)
                        mm.then_inc(k_mm[c], 1)
                else:
                    project(bank2(c, BANK_K[l][0]), l, 1, 0, enc_hi[c], enc_lo[c]).then_inc(k_mm[c], 1)
                    row()
                    pe.wait_ge(nat_rd[c], nth(it, l))
                    project(bank2(c, BANK_K[l][1]), l, 1, 1, enc_hi[c], enc_lo[c]).then_inc(k_mm[c], 1)

            def value_block(c, l, b, bank, half_of_bank):
                t, n = key_blocks(l)[b]
                a_hi, a_lo = (ct_hi, ct_lo) if l == 0 else (enc_hi, enc_lo)
                out = bank2(c, bank)[0:n, half_of_bank, :]
                for k in range(DT):
                    three(out, a_hi[c][:, k, t:t + n], a_lo[c][:, k, t:t + n], w_hi[:, l, 2, k, :], w_lo[:, l, 2, k, :],
                          k == 0, False)
                return pe.matmul(out, ones_r[:, 0:n], bv_split[:, l, :], start=False, stop=True)

            def values_a(c, it, l):
                pe.wait_ge(row_rd[c], nth(it, l))
                value_block(c, l, 0, BANK_VA, 0).then_inc(va_mm[c], 1)

            def values_b(c, it, l):
                if l > 0:
                    pe.wait_ge(p_rd[c], nth(it, l, 2, 2 * HEADS))
                    value_block(c, l, 1, BANK_VB, 0).then_inc(vb_mm[c], 1)

            def scores(c, it, l, s):
                n = T_CTX if l == 0 else S
                for j in ISSUE_ORDER:
                    h = HEAD_OF_SLOT[j]
                    if s == 0 and h % 2 == 0:
                        pe.wait_ge(q_rd[c], nth(it, l, h // 2 + 1, DT))
                        pe.wait_ge(k_rd[h // 2][c], nth(it, l))
                    rows = slice(DH * (h % 2), DH * (h % 2) + DH)
                    mm = pe.matmul(bank2(c, 2 * s + j // 2)[:, j % 2, 0:n], qt[c][rows, h // 2, s * P:(s + 1) * P],
                                   kt[c][rows, h // 2, 0:n], start=True, stop=True)
                    if j % 2 == 1:
                        mm.then_inc(sc_mm[c], 1)

            def scores_a(c, it, l):
                pe.wait_ge(q_rd[c], nth(it, l, DT, DT))
                pe.wait_ge(kraw_rd[c], nth(it, l, 1 if l else DT, DT))
                scores(c, it, l, 0)

            def scores_b(c, it, l):
                pe.wait_ge(nat_rd[c], nth(it, l))
                pe.wait_ge(kraw_rd[c], nth(it, l, DT, DT))
                pe.wait_ge(va_rd[c], nth(it, l))
                scores(c, it, l, 1)

            def turn(c, it, l, slots):
                for j in slots:
                    pe.wait_ge(p_rd[c], nth(it, l, HEADS + j + 1, 2 * HEADS))
                    if BANK_OF_TURN[j] == BANK_VB and l > 0:
                        pe.wait_ge(vb_rd[c], nth_vb(it, l))
                    for b, (t, n) in enumerate(key_blocks(l)):
                        for s in range(ST):
                            mm = pe.transpose(bank2(c, BANK_OF_TURN[j])[0:n, b, s * P:(s + 1) * P], prob[c][:, s, j, t:t + n], ident[:])
                    mm.then_inc(pt_mm[c], 1)

            def turn_a(c, it, l):
                turn(c, it, l, (0, 1))

            def turn_b(c, it, l):
                turn(c, it, l, (2, 3))

            def mix(c, it, l):
                pe.wait_ge(vcol_rd[c], nth(it, l))
                pe.wait_ge(va_rd[c], nth(it, l))
                if l > 0:
                    pe.wait_ge(vb_rd[c], nth_vb(it, l))
                blocks = key_blocks(l)
                for s in range(ST):
                    for j in range(HEADS):
                        h = HEAD_OF_SLOT[j]
                        if s == 0:
                            pe.wait_ge((pta_rd, ptd_rd)[j % 2][c], nth(it, l, j // 2 + 1, 2))
                        for b, (t, n) in enumerate(blocks):
                            mm = pe.matmul(ps[c][:, BANK_MIX + s, h * VH:(h + 1) * VH], prob_t[c][0:n, j, b, s * P:(s + 1) * P],
                                           v[c][0:n, b, h, :], start=b == 0, stop=b == len(blocks) - 1)
                    mm.then_inc(av_mm[c], 1)

            def norm(c, it, l):
                for s in range(ST):
                    pe.wait_ge(z_rd[c], nth(it, l, s + 1, ST))
                    for m in range(DT):
                        mm = pe.transpose(bank2(c, BANK_ZT)[:, m, s * P:(s + 1) * P], z[c][:, s, m * P:(m + 1) * P], ident[:])
                mm.then_inc(zt_mm[c], 1)

            def feed(c, it, l):
                pe.wait_ge(lnhi_rd[c], nth(it, l, DT, DT))
                pe.wait_ge(lnlo_rd[c], nth(it, l, DT, DT))
                for m in range(DT):
                    mm = project(bank2(c, BANK_FF), l, 3, m, ln_hi[c], ln_lo[c])
                mm.then_inc(ff_mm[c], 1)

            steps = dict(align_scores=align_scores, align_turn=align_turn, align_x=align_x, align_out=align_out,
                         natural=natural, queries=queries, keys=keys, values_a=values_a, values_b=values_b, scores_a=scores_a,
                         scores_b=scores_b, turn_a=turn_a, turn_b=turn_b, mix=mix,
                         norm=norm, feed=feed)
            pe.wait_ge(const_in, 64)
            pe.wait_ge(const_rd, 4)
            pe.wait_ge(bias_rd, 3)
            pe.wait_ge(w_split, 2 * (1 + 2 * LAYERS))
            pe.wait_ge(wk0_in, 16)
            run_steps(pe.Fori, lambda name, c, it, l: steps[name](c, it, l) if name in steps else None)

        @block.scalar
        def _(act):
            def col(kind, l, m):
                return cols[:, kind, l, m:m + 1]

            def align_probs(c, it, l):
                act.wait_ge(al_max_rd[c], it + 1)
                for s in range(ST):
                    act.activation(align_e[c][:, s, :], ps[c][:, BANK_AL_SCORES, s * P:s * P + T_CTX], ACT.Exp,
                                   bias=align_nmax[c][:, s:s + 1], accum_out=align_sum[c][:, s:s + 1]).then_inc(al_e_rd[c], 1)
                act.activation(cw[c][0:T_CTX, :], ps[c][0:T_CTX, BANK_AL_SCORES, AL_CW], ACT.Copy).then_inc(cw_rd[c], 1)

            def enc_high(c, it, l):
                for m in range(DT):
                    act.wait_ge(enc_rd[c], nth(it, l, m + 1, DT))
                    act.activation(enc_hi[c][:, m, :], enc_t[c][:, m, :], ACT.Copy).then_inc(enchi_rd[c], 1)

            def align_out(c, it, l):
                for m in range(DT):
                    act.wait_ge(al_x_mm[c], DT * it + m + 1)
                    act.activation(th[c][:, m, :], bank2(c, BANK_AL_X[m])[:, m, :], ACT.Tanh, bias=col(COL_BT, 0, m)).then_inc(th_rd[c], 1)

            def align_encode(c, it, l):
                enc_high(c, it, 0)

            def natural(c, it, l):
                act.wait_ge(nat_mm[c], nth(it, l))
                for s in range(ST):
                    ins = act.activation(enc_n[c][:, s, :], bank2(c, BANK_NATURAL)[:, s, :], ACT.Copy, accum_out=enc_sum[c][:, s:s + 1])
                ins.then_inc(nat_rd[c], 1)

            def queries(c, it, l):
                for m in range(DT):
                    act.wait_ge(q_mm[c], nth(it, l))
                    act.activation(qt[c][:, m, :], bank2(c, BANK_Q)[:, m, :], ACT.Relu, bias=bq_scaled[:, l, m:m + 1],
                                   scale=float(DH) ** -0.5).then_inc(q_rd[c], 1)

            def keys(c, it, l):
                n = T_CTX if l == 0 else S

                act.wait_ge(row_mm[c], nth(it, l))
                for m in range(DT):
                    act.wait_ge(k_rd[m][c], nth(it, l, 0))
                act.activation(keep_row[c][:, 0:n], ps[c][:, BANK_ROW, 0:n], ACT.Copy, accum_out=any_keep[c][:]).then_inc(row_rd[c], 1)
                for m in range(DT):
                    act.wait_ge(k_mm[c], nth(it, l, m + 1 if l else DT, DT))
                    act.activation(kt_raw[c][:, m, 0:n], bank2(c, BANK_K[l][m])[:, m, 0:n], ACT.Relu, bias=col(COL_BK, l, m)
                                   ).then_inc(kraw_rd[c], 1)

            def values_a(c, it, l):
                n = key_blocks(l)[0][1]
                act.wait_ge(keepv_rd[c], nth(it, l))
                act.wait_ge(va_mm[c], nth(it, l))
                act.activation(v[c][0:n, 0, :, 0:DH], bank2(c, BANK_VA)[0:n, 0, :].rearrange("p (h d) -> p h d", h=HEADS), ACT.Relu,
                               scale=keep_v[c][0:n, 0:1]).then_inc(va_rd[c], 1)

            def exps(c, it, l, s, slots):
                n = T_CTX if l == 0 else S
                for j in slots:
                    if j % 2 == 0:
                        act.wait_ge(max_rd[c], nth(it, l, 2 * s + j // 2 + 1, 2 * ST))
                    act.activation(prob[c][:, s, j, 0:n], bank2(c, 2 * s + j // 2)[:, j % 2, 0:n], ACT.Exp,
                                   bias=nmax[c][:, s, j:j + 1]).then_inc(p_rd[c], 1)

            def scores_a(c, it, l):
                if l > 0:
                    exps(c, it, l, 0, (0,))

            def scores_b(c, it, l):
                exps(c, it, l, 0, (1, 2, 3) if l > 0 else range(HEADS))

            def values_b(c, it, l):
                exps(c, it, l, 1, range(HEADS))

            def turn(c, it, l, j):
                n, nb = (T_CTX, 1) if l == 0 else (P, ST)
                act.wait_ge(pt_mm[c], nth(it, l, j + 1, HEADS))
                act.activation(prob_t[c][0:n, j, 0:nb, :], bank2(c, BANK_OF_TURN[j])[0:n, 0:nb, :], ACT.Copy).then_inc(pta_rd[c], 1)

            def turn_a(c, it, l):
                turn(c, it, l, 0)

            def turn_b(c, it, l):
                turn(c, it, l, 2)

            def norm(c, it, l):
                act.wait_ge(zt_mm[c], nth(it, l))
                for m in range(DT):
                    act.activation(ln_t[c][:, m, :], bank2(c, BANK_ZT)[:, m, :], ACT.Identity, bias=col(COL_BETA, l, m),
                                   scale=col(COL_GAMMA, l, m)).then_inc(lnt_rd[c], 1)

            def encode(c, it, l):
                if l < LAYERS - 1:
                    enc_high(c, it, l + 1)

            def align_split(c, it, l):
                act.wait_ge(batch_in[c], it * 48 + 48)
                act.wait_ge(al_x_mm[c], DT * it)
                act.activation(xt_hi[c][:], xt[c][:], ACT.Copy).then_inc(x_split[c], 1)

            def feed(c, it, l):
                act.wait_ge(ff_mm[c], nth(it, l))
                for m in range(DT):
                    ins = act.activation(ff[c][:, m, :], bank2(c, BANK_FF)[:, m, :], ACT.Identity, bias=col(COL_BFF, l, m))
                ins.then_inc(u_rd[c], 1)

            steps = dict(align_split=align_split, align_probs=align_probs, align_out=align_out, align_encode=align_encode, natural=natural, keys=keys, queries=queries,
                         values_a=values_a, scores_a=scores_a, scores_b=scores_b, values_b=values_b, turn_a=turn_a, turn_b=turn_b, norm=norm, feed=feed, encode=encode)
            act.wait_ge(const_in, 64)
            act.wait_ge(const_rd, 4)
            run_steps(act.Fori, lambda name, c, it, l: steps[name](c, it, l) if name in steps else None)

        @block.gpsimd
        def _(pool):
            def spread(c, it, l):
                pool.wait_ge(var_rd[c], nth(it, l, 2, ST))
                pool.tensor_tensor(std[c][:], var[c][:], half[:], ALU.pow).then_inc(std_rd[c], 1)

            def align_split_low(c, it, l):
                pool.wait_ge(x_split[c], 2 * it + 1)
                pool.tensor_tensor(xt_lo[c][:], xt[c][:], xt_hi[c][:].bitcast(F32), ALU.subtract).then_inc(x_split[c], 1)

            def keys(c, it, l):
                n = T_CTX if l == 0 else S
                pool.wait_ge(kraw_rd[c], nth(it, l, 2, DT))
                pool.wait_ge(row_rd[c], nth(it, l))
                pool.tensor_tensor(kt[c][:, 1, 0:n], kt_raw[c][:, 1, 0:n], keep_row[c][:, 0:n], ALU.mult).then_inc(k_rd[1][c], 1)

            def enc_low(c, it, l):
                for m in range(DT):
                    pool.wait_ge(enchi_rd[c], nth(it, l, m + 1, DT))
                    pool.tensor_tensor(enc_lo[c][:, m, :], enc_t[c][:, m, :], enc_hi[c][:, m, :].bitcast(F32), ALU.subtract
                                       ).then_inc(enclo_rd[c], 1)

            def encode(c, it, l):
                last = l == LAYERS - 1
                if last:
                    pool.wait_ge(out_sent[c], 16 * it)
                for m in range(DT):
                    pool.wait_ge(ffl_rd[c], nth(it, l, m + 1, DT))
                    pool.tensor_tensor((final if last else enc_t)[c][:, m, :], ff[c][:, m, :], ln_t[c][:, m, :], ALU.add
                                       ).then_inc((final_rd if last else enc_rd)[c], 1)
                if not last:
                    enc_low(c, it, l + 1)

            def align_out(c, it, l):
                for m in range(DT):
                    pool.wait_ge(th_rd[c], DT * it + m + 1)
                    pool.tensor_tensor(enc_t[c][:, m, :], th[c][:, m, :], xt[c][:, m, :], ALU.add).then_inc(enc_rd[c], 1)

            def align_encode(c, it, l):
                enc_low(c, it, 0)

            pool.wait_ge(const_rd, 4)
            steps = dict(keys=keys, spread=spread, encode=encode, align_split_low=align_split_low, align_out=align_out, align_encode=align_encode)
            run_steps(pool.Fori, lambda name, c, it, l: steps[name](c, it, l) if name in steps else None)

        @block.vector
        def _(dve):
            dve.memset(ones_f[:], 1.0).then_inc(bias_rd, 1)
            dve.memset(half[:], 0.5).then_inc(const_rd, 1)
            for c in CHAINS:
                dve.memset(ct_hi[c][:].bitcast(F32), 0.0).then_inc(pad_rd, 1)
                dve.memset(ct_lo[c][:].bitcast(F32), 0.0).then_inc(pad_rd, 1)
            dve.memset(bv_split[:].bitcast(F32), 0.0).then_inc(pad_rd, 1)
            dve.wait_ge(const_in, 64)
            dve.tensor_copy(ident_bf[:], ident[:]).then_inc(const_rd, 1)
            dve.tensor_scalar(bq_scaled[:], cols[:, COL_BQ], float(DH) ** -0.5, None, ALU.mult).then_inc(const_rd, 1)
            dve.wait_ge(bias_rd, 1)
            dve.tensor_copy(ones_r[:], ones_f[:]).then_inc(const_rd, 1)
            dve.tensor_copy(bv_hi[32:33], bv[32:33]).then_inc(pad_rd, 1)
            dve.wait_ge(pad_rd, 6)
            dve.tensor_copy(bv_split[0:1], bv[0:1]).then_inc(bias_rd, 1)
            dve.tensor_tensor(bv_split[32:33], bv[32:33], bv_hi[32:33].bitcast(F32), ALU.subtract).then_inc(bias_rd, 1)
            dests = [(wa_hi[:], wa_lo[:])]
            for l in range(LAYERS):
                for pair in range(2):
                    dests.append(tuple(w[:, l, 2 * pair:2 * pair + 2].rearrange("p w k n -> p (w k) n") for w in (w_hi, w_lo)))
            for n, (hi, lo) in enumerate(dests):
                dve.wait_ge(w_in[n % 2], 16 * (n // 2 + 1))
                dve.tensor_copy(hi, stage_w[:, n % 2]).then_inc(w_split, 1)
                dve.wait_ge(w_split, 2 * n + 1)
                dve.tensor_tensor(lo, stage_w[:, n % 2], hi.bitcast(F32), ALU.subtract).then_inc(w_split, 1)

            def align_split(c, it, l):
                dve.wait_ge(batch_in[c], it * 48 + 48)
                dve.wait_ge(pad_rd, 6)
                if not first_batch(it):
                    dve.wait_ge(va_mm[c], nth(it, 0) - LAYERS)
                dve.tensor_copy(ct_hi[c][:, :, 0:T_CTX], ct[c][:, :, 0:T_CTX]).then_inc(ct_split[c], 1)
                dve.tensor_reduce(c_sum[c][0:T_CTX], cn[c][0:T_CTX, :], AX.X, ALU.add).then_inc(csum_rd[c], 1)
                dve.wait_ge(ct_split[c], 2 * it + 1)
                dve.tensor_tensor(ct_lo[c][:, :, 0:T_CTX], ct[c][:, :, 0:T_CTX], ct_hi[c][:, :, 0:T_CTX].bitcast(F32),
                                  ALU.subtract).then_inc(ct_split[c], 1)

            def align_probs(c, it, l):
                dve.wait_ge(al_sc_mm[c], it + 1)
                dve.tensor_reduce(align_nmax[c][:], ps[c][:, BANK_AL_SCORES, 0:S].rearrange("p (s t) -> p s t", s=ST)[:, :, 0:T_CTX], AX.X,
                                  ALU.max, negate=True).then_inc(al_max_rd[c], 1)
                dve.wait_ge(al_e_rd[c], 2 * it + 2)
                dve.reciprocal(align_rsum[c][:], align_sum[c][:]).then_inc(al_rs_rd[c], 1)
                dve.wait_ge(al_rs_rd[c], it + 1)
                dve.tensor_tensor(align_p[c][:], align_e[c][:], align_rsum[c][:].unsqueeze(2).broadcast_to([P, ST, T_CTX]),
                                  ALU.mult).then_inc(al_p_rd[c], 1)

            def align_out(c, it, l):
                dve.wait_ge(csum_rd[c], it + 1)
                for out in (keep_bf, keep_k):
                    dve.tensor_scalar(out[c][0:T_CTX, 0:1], c_sum[c][0:T_CTX], 0.0, None, ALU.not_equal).then_inc(keepk_rd[c], 1)

            def align_turn(c, it, l):
                dve.wait_ge(al_pt_mm[c], it + 1)
                dve.tensor_copy(align_pt[c][0:T_CTX, :], ps[c][0:T_CTX, BANK_AL_SCORES, 0:S]).then_inc(al_pt_rd[c], 1)

            def natural(c, it, l):
                dve.wait_ge(nat_rd[c], nth(it, l))
                if l > 0:
                    for out in (keep_bf, keep_k):
                        dve.tensor_scalar(out[c][:], enc_sum[c][:], 0.0, None, ALU.not_equal).then_inc(keepk_rd[c], 1)
                dve.tensor_scalar(keep_q[c][:], enc_sum[c][:], 0.0, None, ALU.not_equal).then_inc(keepq_rd[c], 1)

            def keys(c, it, l):
                n, nb, keys = (T_CTX, 1, T_CTX) if l == 0 else (P, ST, S)
                dve.wait_ge(keepk_rd[c], 2 * nth(it, l))
                dve.wait_ge(row_rd[c], nth(it, l))
                dve.tensor_scalar(none_keep[c][:], any_keep[c][:], 0.0, None, ALU.is_equal).then_inc(none_rd[c], 1)
                dve.wait_ge(kraw_rd[c], nth(it, l, 1, DT))
                dve.tensor_tensor(kt[c][:, 0, 0:keys], kt_raw[c][:, 0, 0:keys], keep_row[c][:, 0:keys], ALU.mult).then_inc(k_rd[0][c], 1)
                dve.wait_ge(none_rd[c], nth(it, l))
                dve.tensor_scalar(keep_v[c][0:n, 0:nb], keep_k[c][0:n, 0:nb], none_keep[c][0:n, 0:1], None,
                                  ALU.max).then_inc(keepv_rd[c], 1)
                dve.wait_ge(keepv_rd[c], nth(it, l))
                dve.tensor_copy(v[c][0:n, 0:nb, :, DH], keep_v[c][0:n, 0:nb].unsqueeze(2).broadcast_to([n, nb, HEADS])
                                ).then_inc(vcol_rd[c], 1)

            def maxes(c, it, l, bank):
                n = T_CTX if l == 0 else S
                dve.wait_ge(sc_mm[c], nth(it, l, bank + 1, 2 * ST))
                dve.tensor_reduce(nmax[c][:, bank // 2, 2 * (bank % 2):2 * (bank % 2) + 2], bank2(c, bank)[:, :, 0:n],
                                  AX.X, ALU.max, negate=True).then_inc(max_rd[c], 1)

            def scores_a(c, it, l):
                maxes(c, it, l, 0)
                maxes(c, it, l, 1)

            def scores_b(c, it, l):
                maxes(c, it, l, 2)

            def values_b(c, it, l):
                maxes(c, it, l, 3)
                if l > 0:
                    dve.wait_ge(vb_mm[c], nth_vb(it, l))
                    dve.tensor_scalar(v[c][:, 1, :, 0:DH], bank2(c, BANK_VB)[:, 0, :].rearrange("p (h d) -> p h d", h=HEADS),
                                      keep_v[c][:, 1:2], 0.0, ALU.mult, ALU.max).then_inc(vb_rd[c], 1)

            def turn(c, it, l, j):
                n, nb = (T_CTX, 1) if l == 0 else (P, ST)
                dve.wait_ge(pt_mm[c], nth(it, l, j + 1, HEADS))
                dve.tensor_copy(prob_t[c][0:n, j, 0:nb, :], bank2(c, BANK_OF_TURN[j])[0:n, 0:nb, :]).then_inc(ptd_rd[c], 1)

            def turn_a(c, it, l):
                turn(c, it, l, 1)

            def turn_b(c, it, l):
                turn(c, it, l, 3)

            def stats(c, it, l, s):
                dve.wait_ge(res_rd[c], nth(it, l, s + 1, ST))
                dve.bn_stats(bn[c][:, s, :], res[c][:, s, :]).then_inc(bn_rd[c], 1)

            def variance(c, it, l, s):
                dve.wait_ge(mv_rd[c], nth(it, l, s + 1, ST))
                dve.tensor_scalar(var[c][:, s:s + 1], mv[c][:, s, 1:2], D / (D - 1.0), None, ALU.mult).then_inc(var_rd[c], 1)

            def mix(c, it, l):
                att_h = att[c][:].rearrange("p s (h d) -> p s h d", h=HEADS)

                def mixed(s):
                    return ps[c][:, BANK_MIX + s, 0:HEADS * VH].rearrange("p (h d) -> p h d", h=HEADS)

                def denominators(s):
                    dve.wait_ge(av_mm[c], nth(it, l, s + 1, ST))
                    dve.reciprocal(rsum[c][:, s], mixed(s)[:, :, DH]).then_inc(rsum_rd[c], 1)

                def factors(s):
                    dve.wait_ge(rsum_rd[c], nth(it, l, s + 1, ST))
                    dve.tensor_scalar(rscale[c][:, s], rsum[c][:, s], keep_q[c][:, s:s + 1], None, ALU.mult).then_inc(rscale_rd[c], 1)

                def attended(s):
                    dve.wait_ge(rscale_rd[c], nth(it, l, s + 1, ST))
                    dve.tensor_tensor(att_h[:, s], mixed(s)[:, :, 0:DH], rscale[c][:, s].unsqueeze(2).broadcast_to([P, HEADS, DH]),
                                      ALU.mult).then_inc(att_rd[c], 1)

                def add_input(s):
                    dve.wait_ge(att_rd[c], nth(it, l, s + 1, ST))
                    dve.tensor_tensor(res[c][:, s, :], att[c][:, s, :], enc_n[c][:, s, :], ALU.add).then_inc(res_rd[c], 1)

                denominators(0)
                dve.wait_ge(keepq_rd[c], nth(it, l))
                factors(0)
                attended(0)
                add_input(0)
                denominators(1)
                stats(c, it, l, 0)
                factors(1)
                attended(1)
                dve.wait_ge(bn_rd[c], nth(it, l, 1, ST))
                add_input(1)
                dve.bn_aggr(mv[c][:, 0, :], bn[c][:, 0, :]).then_inc(mv_rd[c], 1)

            def spread(c, it, l):
                stats(c, it, l, 1)
                dve.wait_ge(bn_rd[c], nth(it, l, 2, ST))
                variance(c, it, l, 0)
                dve.bn_aggr(mv[c][:, 1, :], bn[c][:, 1, :]).then_inc(mv_rd[c], 1)
                variance(c, it, l, 1)

            def center(c, it, l):
                dve.wait_ge(std_rd[c], nth(it, l))
                dve.tensor_scalar(std_eps[c][:], std[c][:], EPS, None, ALU.add).then_inc(stde_rd[c], 1)
                dve.wait_ge(stde_rd[c], nth(it, l))
                dve.reciprocal(rstd[c][:], std_eps[c][:]).then_inc(rstd_rd[c], 1)
                dve.wait_ge(rstd_rd[c], nth(it, l))
                for s in range(ST):
                    dve.tensor_scalar(z[c][:, s, :], res[c][:, s, :], mv[c][:, s, 0:1], rstd[c][:, s:s + 1], ALU.subtract,
                                      ALU.mult).then_inc(z_rd[c], 1)

            def norm_parts(c, it, l):
                for m in range(DT):
                    dve.wait_ge(lnt_rd[c], nth(it, l, m + 1, DT))
                    dve.tensor_copy(ln_hi[c][:, m, :], ln_t[c][:, m, :]).then_inc(lnhi_rd[c], 1)
                    dve.wait_ge(lnhi_rd[c], nth(it, l, m + 1, DT))
                    dve.tensor_tensor(ln_lo[c][:, m, :], ln_t[c][:, m, :], ln_hi[c][:, m, :].bitcast(F32), ALU.subtract
                                      ).then_inc(lnlo_rd[c], 1)

            def leak(c, it, l, m):
                dve.wait_ge(u_rd[c], nth(it, l))
                dve.scalar_tensor_tensor(ff[c][:, m, :], ff[c][:, m, :], LEAK, ff[c][:, m, :], ALU.mult, ALU.max).then_inc(ffl_rd[c], 1)

            def leak_a(c, it, l):
                leak(c, it, l, 0)

            def leak_b(c, it, l):
                leak(c, it, l, 1)

            steps = dict(align_split=align_split, align_probs=align_probs, align_turn=align_turn, align_out=align_out,
                         natural=natural, keys=keys, spread=spread, values_b=values_b, scores_a=scores_a,
                         scores_b=scores_b, turn_a=turn_a, turn_b=turn_b, mix=mix,
                         center=center, norm_parts=norm_parts, leak_a=leak_a, leak_b=leak_b)
            run_steps(dve.Fori, lambda name, c, it, l: steps[name](c, it, l) if name in steps else None)


def columns_of(vectors):
    n, layers, d = vectors.shape
    return np.ascontiguousarray(vectors.reshape(n, layers, d // P, P).transpose(3, 0, 1, 2))


def kernel(**inputs):
    import concourse.bacc as bacc
    from concourse.bass_utils import run_bass_kernel_spmd

    a = {k: np.asarray(x) for k, x in inputs.items()}
    bt = a["L0_xattn_trans_b"]
    arrays = {
        "x_t": np.ascontiguousarray(a["x"].transpose(0, 2, 1)),
        "ctx_t": np.ascontiguousarray(a["ctx_1024"].transpose(0, 2, 1)),
        "ctx_n": np.ascontiguousarray(a["ctx_1024"]),
        "w_align": np.ascontiguousarray(a["L0_xattn_trans_W"]),
        "w_qkvf": np.ascontiguousarray(np.stack([a["L1_xattn_Wq"], a["L1_xattn_Wk"], a["L1_xattn_Wv"], a["L1_xattn_Wff"]], 1)),
        "columns": columns_of(np.stack([a["L1_xattn_bq"], a["L1_xattn_bk"], a["L1_xattn_gamma"], a["L1_xattn_beta"],
                                        a["L1_xattn_bff"], np.stack([bt] * LAYERS)])),
        "bv_row": np.ascontiguousarray(a["L1_xattn_bv"][None]),
        "identity": np.eye(P, dtype=np.float32),
    }
    nc = bacc.Bacc("TRN2", target_bir_lowering=False, num_devices=1)
    aps = [nc.dram_tensor(f"in_{n}", x.shape, mybir.dt.from_np(x.dtype), kind="ExternalInput").ap() for n, x in arrays.items()]
    b, s, d = a["x"].shape
    out = nc.dram_tensor("out_t", (b, d, s), F32, kind="ExternalOutput").ap()
    build_program(nc, *aps, out)
    r = run_bass_kernel_spmd(nc, [{f"in_{n}": x for n, x in arrays.items()}], core_ids=[0])
    return np.ascontiguousarray(r.results[0]["out_t"].transpose(0, 2, 1))
```

```python
from contextlib import ExitStack

import numpy as np

import concourse.bass as bass
from concourse import mybir

ALU = mybir.AluOpType
ACT = mybir.ActivationFunctionType
AX = mybir.AxisListType
F32 = mybir.dt.float32
F32R = mybir.dt.float32r
BF16 = mybir.dt.bfloat16

P = 128
LAYERS = 3
HEADS = 4
EPS = 1e-8
LEAK = 0.2
COL_BQ, COL_BK, COL_GAMMA, COL_BETA, COL_BFF, COL_BT = 0, 1, 2, 3, 4, 5
HEAD_OF_SLOT = [0, 2, 1, 3]
ISSUE_ORDER = [0, 2, 1, 3]
TURN_ORDER = [0, 1, 3, 2]


def build_program(nc, x_t, ctx_t, ctx_n, w_align, w_qkvf, columns, bv_row, identity, out_t):
    batches, D, S = x_t.shape
    T_CTX = ctx_n.shape[1]
    DT = D // P
    ST = S // P
    DH = D // HEADS
    ROUNDS = batches // 2
    CTX_PAD = T_CTX + T_CTX % 2
    VH = DH + 1
    assert D == 2 * P and S == 2 * P and DH == 64 and batches % 2 == 0 and T_CTX < P
    CHAINS = range(2)

    with ExitStack() as ctx:
        def sb(name, shape, dt=F32):
            return ctx.enter_context(nc.sbuf_tensor(name, shape, dt))

        def sb2(name, shape, dt=F32):
            return [sb(f"{name}_{c}", shape, dt) for c in "ab"]

        def sem(name):
            return ctx.enter_context(nc.semaphore(name))

        def sem2(name):
            return [sem(f"{name}_{c}") for c in "ab"]

        stage_w = sb("stage_w", [P, 2, 4, D])
        wa_hi = sb("wa_hi", [P, 2 * DT, D], F32R)
        wa_lo = sb("wa_lo", [P, 2 * DT, D], F32R)
        w_hi = sb("w_hi", [P, LAYERS, 4, DT, D], F32R)
        w_lo = sb("w_lo", [P, LAYERS, 4, DT, D], F32R)
        wk0 = sb("wk0", [P, DT, D])
        cols = sb("cols", [P, 6, LAYERS, DT])
        bk_scaled = sb("bk_scaled", [P, LAYERS, DT])
        ident = sb("ident", [P, P])
        ident_bf = sb("ident_bf", [P, P], BF16)
        ones_f = sb("ones_f", [P, P])
        ones_r = sb("ones_r", [P, P], F32R)
        half = sb("half", [P, ST])
        bv = sb("bv", [P, LAYERS, D])
        bv_hi = sb("bv_hi", [P, LAYERS, D], F32R)
        bv_split = sb("bv_split", [P, LAYERS, D], F32R)

        xt = sb2("xt", [P, DT, S])
        xt_hi = sb2("xt_hi", [P, DT, S], F32R)
        xt_lo = sb2("xt_lo", [P, DT, S], F32R)
        ct = sb2("ct", [P, DT, CTX_PAD])
        ct_hi = sb2("ct_hi", [P, DT, CTX_PAD], F32R)
        ct_lo = sb2("ct_lo", [P, DT, CTX_PAD], F32R)
        cn = sb2("cn", [P, D])
        c_sum = sb2("c_sum", [P, 1])
        align_nmax = sb2("align_nmax", [P, ST])
        align_sum = sb2("align_sum", [P, ST])
        align_rsum = sb2("align_rsum", [P, ST])
        align_e = sb2("align_e", [P, ST, T_CTX])
        align_p = sb2("align_p", [P, ST, T_CTX])
        align_pt = sb2("align_pt", [P, S])
        cw = sb2("cw", [P, D])
        th = sb2("th", [P, DT, S])
        enc_t = sb2("enc_t", [P, DT, S])
        enc_hi = sb2("enc_hi", [P, DT, S], F32R)
        enc_lo = sb2("enc_lo", [P, DT, S], F32R)
        final = sb2("final", [P, DT, S])
        enc_n = sb2("enc_n", [P, ST, D])
        enc_sum = sb2("enc_sum", [P, ST])
        keep_q = sb2("keep_q", [P, ST])
        keep_k = sb2("keep_k", [P, ST])
        keep_bf = sb2("keep_bf", [P, ST], BF16)
        keep_row = sb2("keep_row", [P, S])
        any_keep = sb2("any_keep", [P, 1])
        none_keep = sb2("none_keep", [P, 1])
        keep_v = sb2("keep_v", [P, ST])
        qt = sb2("qt", [P, DT, S])
        kt_raw = sb2("kt_raw", [P, DT, S])
        kt = sb2("kt", [P, DT, S])
        v = sb2("v", [P, ST, HEADS, VH])
        nmax = sb2("nmax", [P, ST, HEADS])
        prob = sb2("prob", [P, ST, HEADS, S])
        prob_t = sb2("prob_t", [P, HEADS, ST, S])
        rsum = sb2("rsum", [P, ST, HEADS])
        rscale = sb2("rscale", [P, ST, HEADS])
        att = sb2("att", [P, ST, D])
        res = sb2("res", [P, ST, D])
        bn = sb2("bn", [P, ST, 6])
        mv = sb2("mv", [P, ST, 2])
        var = sb2("var", [P, ST])
        std = sb2("std", [P, ST])
        std_eps = sb2("std_eps", [P, ST])
        rstd = sb2("rstd", [P, ST])
        z = sb2("z", [P, ST, D])
        ln_t = sb2("ln_t", [P, DT, S])
        ln_hi = sb2("ln_hi", [P, DT, S], F32R)
        ln_lo = sb2("ln_lo", [P, DT, S], F32R)
        ff = sb2("ff", [P, DT, S])

        ps = [ctx.enter_context(nc.psum_tensor(f"ps_{c}", [P, 4, 512], F32)) for c in "ab"]

        const_in = sem("const_in")
        w_in = [sem(f"w_in_{n}") for n in range(2)]
        wk0_in = sem("wk0_in")
        w_split = sem("w_split")
        const_rd = sem("const_rd")
        bias_rd = sem("bias_rd")
        pad_rd = sem("pad_rd")
        batch_in = sem2("batch_in")
        out_sent = sem2("out_sent")
        al_sc_mm, al_pt_mm, al_x_mm = (sem2(s) for s in ("al_sc_mm", "al_pt_mm", "al_x_mm"))
        nat_mm, q_mm, k_mm, row_mm = (sem2(s) for s in ("nat_mm", "q_mm", "k_mm", "row_mm"))
        va_mm, vb_mm = (sem2(s) for s in ("va_mm", "vb_mm"))
        sc_mm, pt_mm, av_mm, zt_mm, ff_mm = (sem2(s) for s in ("sc_mm", "pt_mm", "av_mm", "zt_mm", "ff_mm"))
        al_e_rd, cw_rd, th_rd = (sem2(s) for s in ("al_e_rd", "cw_rd", "th_rd"))
        nat_rd, kraw_rd, p_rd = (sem2(s) for s in ("nat_rd", "kraw_rd", "p_rd"))
        q_rd = [sem2(f"q{m}_rd") for m in range(DT)]
        pta_rd, lnt_rd, u_rd = (sem2(s) for s in ("pta_rd", "lnt_rd", "u_rd"))
        x_split, ct_split, csum_rd = (sem2(s) for s in ("x_split", "ct_split", "csum_rd"))
        al_max_rd, al_rs_rd, al_p_rd, al_pt_rd = (sem2(s) for s in ("al_max_rd", "al_rs_rd", "al_p_rd", "al_pt_rd"))
        keepq_rd, keepk_rd, row_rd, none_rd = (sem2(s) for s in ("keepq_rd", "keepk_rd", "row_rd", "none_rd"))
        keepv_rd, vcol_rd, max_rd, ptd_rd = (sem2(s) for s in ("keepv_rd", "vcol_rd", "max_rd", "ptd_rd"))
        rsum_rd, rscale_rd, att_rd, res_rd, bn_rd = (sem2(s) for s in ("rsum_rd", "rscale_rd", "att_rd", "res_rd", "bn_rd"))
        va_rd, vb_rd = (sem2(s) for s in ("va_rd", "vb_rd"))
        mv_rd, var_rd, stde_rd, rstd_rd, z_rd = (sem2(s) for s in ("mv_rd", "var_rd", "stde_rd", "rstd_rd", "z_rd"))
        lnhi_rd, ffl_rd, enc_rd, enchi_rd, final_rd = (sem2(s) for s in ("lnhi_rd", "ffl_rd", "enc_rd", "enchi_rd", "final_rd"))
        lnlo_rd, enclo_rd = (sem2(s) for s in ("lnlo_rd", "enclo_rd"))
        k_rd = [sem2(f"k{m}_rd") for m in range(DT)]
        std_rd = sem2("std_rd")

        def nth(it, l, j=1, per=1):
            return it * (LAYERS * per) + (l * per + j)

        def first_batch(it):
            return isinstance(it, int) and it == 0

        def last_batch(it):
            return isinstance(it, int) and it == ROUNDS - 1

        def nth_vb(it, l):
            return it * (LAYERS - 1) + l

        def key_blocks(l):
            return [(0, T_CTX)] if l == 0 else [(s * P, P) for s in range(ST)]

        def bank2(c, b):
            return ps[c][:, b].rearrange("p (m s) -> p m s", m=2)

        BANK_Q, BANK_NATURAL, BANK_ROW = 0, 2, 3
        BANK_K = [[1, 1]] + [[1, 2]] * (LAYERS - 1)
        BANK_VA, BANK_VB, BANK_ZT, BANK_FF = 3, 0, 0, 3
        BANK_OF_TURN = [1, 2, 0, 3]
        BANK_MIX = 1
        BANK_AL_SCORES = 1
        BANK_AL_X = [2, 0]
        AL_CW = slice(D, 2 * D)

        def run_steps(fori, do):
            A, B = 0, 1

            def tail(c, l, it):
                late = dict(turn_b=["encode"]) if l < LAYERS - 1 else dict(mix=["encode"])
                return dict(first=["spread"], keys=["center"], scores_a=["norm"], scores_rest=["norm_parts"],
                            values_b=["feed"], turn_a=["leak"], **late), c, l, it

            def split(c, it):
                return dict(turn_b=["align_split"], mix=["align_split_low"]), c, 0, it

            def align_b(it):
                return dict(queries=["align_scores"], values_a=["align_probs"], scores_b=["align_x", "align_turn"],
                            values_b=["align_out"], turn_b=["align_encode"]), B, 0, it

            def align_a_attention(it):
                return dict(scores_b=["align_scores"], values_b=["align_probs"], turn_b=["align_turn"]), A, 0, it

            def align_a_output(it):
                return dict(scores_b=["align_x"], values_b=["align_out"], turn_b=["align_encode"]), A, 0, it

            def attention(c, l, it, *between):
                def others(name):
                    for places, c2, l2, it2 in between:
                        for other in places.get(name, []):
                            do(other, c2, it2, l2)

                for name in ["natural", "queries", "keys", "values_a", "scores_a", "scores_rest", "scores_b", "values_b",
                             "turn_a", "turn_b", "mix"]:
                    do(name, c, it, l)
                    if name == ("natural" if l else "queries"):
                        others("first")
                    others(name)

            def alone(*groups):
                for places, c, l, it in groups:
                    for names in places.values():
                        for name in names:
                            do(name, c, it, l)

            def chain_round(it, it_before, last):
                coming = [] if last else [it + 1]
                before = [] if it_before is None else [it_before]
                attention(A, 0, it, *[tail(B, 2, i) for i in before], align_b(it), *[split(A, i) for i in coming])
                attention(B, 0, it, *[align_a_attention(i) for i in coming], tail(A, 0, it))
                attention(A, 1, it, tail(B, 0, it))
                attention(B, 1, it, tail(A, 1, it))
                attention(A, 2, it, tail(B, 1, it))
                attention(B, 2, it, tail(A, 2, it), *[align_a_output(i) for i in coming], *[split(B, i) for i in coming])

            alone(split(A, 0), align_a_attention(0), align_a_output(0), split(B, 0))
            chain_round(0, None, False)
            with fori(0, ROUNDS - 2) as it:
                chain_round(it + 1, it, False)
            chain_round(ROUNDS - 1, ROUNDS - 2, True)
            alone(tail(B, 2, ROUNDS - 1))

        block = ctx.enter_context(nc.Block())

        @block.sync
        def _(sp):
            def load(c, b):
                sp.dma_start(xt[c][:], x_t[b].rearrange("(k p) s -> p k s", p=P)).then_inc(batch_in[c], 16)
                sp.dma_start(ct[c][:, :, 0:T_CTX], ctx_t[b].rearrange("(k p) s -> p k s", p=P)).then_inc(batch_in[c], 16)
                sp.dma_start(cn[c][0:T_CTX, :], ctx_n[b]).then_inc(batch_in[c], 16)

            sp.dma_start(cols[:], columns).then_inc(const_in, 16)
            sp.dma_start(ident[:], identity).then_inc(const_in, 16)
            sp.dma_start(bv[0:1], bv_row).then_inc(const_in, 16)
            sp.dma_start(bv[32:33], bv_row).then_inc(const_in, 16)
            sp.dma_start(stage_w[:, 0], w_align.rearrange("(k p) n -> p k n", p=P)).then_inc(w_in[0], 16)
            for c in CHAINS:
                load(c, c)
            n = 1
            for l in range(LAYERS):
                for pair in range(2):
                    if n >= 2:
                        sp.wait_ge(w_split, 2 * (n - 1))
                    sp.dma_start(stage_w[:, n % 2].rearrange("p (w k) n -> p w k n", w=2),
                                 w_qkvf[l, 2 * pair:2 * pair + 2].rearrange("w (k p) n -> p w k n", p=P)).then_inc(w_in[n % 2], 16)
                    n += 1
            sp.dma_start(wk0[:], w_qkvf[0, 1].rearrange("(k p) n -> p k n", p=P)).then_inc(wk0_in, 16)

            def next_batch(c, it):
                sp.wait_ge(enc_rd[c], nth(it, 0, DT, DT))
                sp.wait_ge(k_mm[c], nth(it, 0, DT, DT))
                sp.wait_ge(va_mm[c], nth(it, 0))
                load(c, (it + 1) * 2 + c)

            def store(c, it):
                sp.wait_ge(final_rd[c], DT * it + DT)
                sp.dma_start(out_t[it * 2 + c].rearrange("(k p) s -> p k s", p=P), final[c][:]).then_inc(out_sent[c], 16)

            A, B = CHAINS
            next_batch(A, 0)
            next_batch(B, 0)
            store(A, 0)
            with sp.Fori(0, ROUNDS - 2) as it:
                next_batch(A, it + 1)
                store(B, it)
                next_batch(B, it + 1)
                store(A, it + 1)
            store(B, ROUNDS - 2)
            store(A, ROUNDS - 1)
            store(B, ROUNDS - 1)
            for c in CHAINS:
                sp.wait_ge(out_sent[c], 16 * ROUNDS)

        @block.tensor
        def _(pe):
            def three(out, a_hi, a_lo, b_hi, b_lo, first, last):
                pe.matmul(out, a_hi, b_hi, start=first, stop=False)
                pe.matmul(out, a_hi, b_lo, start=False, stop=False)
                return pe.matmul(out, a_lo, b_hi, start=False, stop=last)

            def project(out, l, w, m, hi, lo):
                for k in range(DT):
                    mm = three(out[:, m, :], w_hi[:, l, w, k, m * P:(m + 1) * P], w_lo[:, l, w, k, m * P:(m + 1) * P],
                               hi[:, k, :], lo[:, k, :], k == 0, k == DT - 1)
                return mm

            def align_scores(c, it, l):
                pe.wait_ge(batch_in[c], it * 48 + 48)
                pe.wait_ge(ct_split[c], 2 * it + 2)
                pe.wait_ge(att_rd[c], nth(it, 0, 0, ST) - (0 if c == 1 or first_batch(it) else ST * (LAYERS - 1)))
                for k in range(DT):
                    three(ps[c][0:T_CTX, BANK_AL_SCORES, AL_CW], ct_hi[c][:, k, 0:T_CTX], ct_lo[c][:, k, 0:T_CTX],
                          wa_hi[:, DT + k, :], wa_lo[:, DT + k, :], k == 0, k == DT - 1)
                for s in range(ST):
                    for k in range(DT):
                        mm = pe.matmul(ps[c][:, BANK_AL_SCORES, s * P:s * P + T_CTX], xt[c][:, k, s * P:(s + 1) * P],
                                       ct[c][:, k, 0:T_CTX], start=k == 0, stop=k == DT - 1)
                mm.then_inc(al_sc_mm[c], 1)

            def align_turn(c, it, l):
                pe.wait_ge(al_p_rd[c], it + 1)
                pe.wait_ge(cw_rd[c], it + 1)
                for s in range(ST):
                    mm = pe.transpose(ps[c][0:T_CTX, BANK_AL_SCORES, s * P:(s + 1) * P], align_p[c][:, s, :], ident[:])
                mm.then_inc(al_pt_mm[c], 1)

            def align_x(c, it, l):
                pe.wait_ge(x_split[c], 2 * it + 2)
                pe.wait_ge(att_rd[c], nth(it, 0, 0, ST))
                for m in range(DT):
                    if m == 1:
                        pe.wait_ge(lnt_rd[c], nth(it, 0, 0, DT))
                    for k in range(DT):
                        three(bank2(c, BANK_AL_X[m])[:, m, :], wa_hi[:, k, m * P:(m + 1) * P], wa_lo[:, k, m * P:(m + 1) * P],
                              xt_hi[c][:, k, :], xt_lo[c][:, k, :], k == 0, False)

            def align_out(c, it, l):
                pe.wait_ge(al_pt_rd[c], it + 1)
                for m in range(DT):
                    pe.matmul(bank2(c, BANK_AL_X[m])[:, m, :], cw[c][0:T_CTX, m * P:(m + 1) * P], align_pt[c][0:T_CTX, :],
                              start=False, stop=True).then_inc(al_x_mm[c], 1)

            def natural(c, it, l):
                pe.wait_ge(enc_rd[c], nth(it, l, DT, DT))
                for s in range(ST):
                    for m in range(DT):
                        mm = pe.transpose(bank2(c, BANK_NATURAL)[:, s, m * P:(m + 1) * P], enc_t[c][:, m, s * P:(s + 1) * P], ident[:])
                mm.then_inc(nat_mm[c], 1)

            def queries(c, it, l):
                pe.wait_ge(enclo_rd[c], nth(it, l, DT, DT))
                for m in range(DT):
                    mm = project(bank2(c, BANK_Q), l, 0, m, enc_hi[c], enc_lo[c])
                mm.then_inc(q_mm[c], 1)

            def keys(c, it, l):
                def row():
                    if l == 0:
                        pe.wait_ge(u_rd[c], nth(it, l, 0))
                    pe.wait_ge(keepk_rd[c], 2 * nth(it, l))
                    for b, (t, n) in enumerate(key_blocks(l)):
                        mm = pe.matmul(ps[c][:, BANK_ROW, t:t + n], keep_bf[c][0:n, b:b + 1].broadcast_to([n, P]), ident_bf[0:n, 0:n],
                                       start=True, stop=True)
                    mm.then_inc(row_mm[c], 1)

                if l == 0:
                    pe.wait_ge(al_pt_rd[c], it + 1)
                if c == 0 and l == 1 and not last_batch(it):
                    pe.wait_ge(al_pt_rd[c], it + 2)
                if l == 0:
                    row()
                    for m in range(DT):
                        for k in range(DT):
                            mm = pe.matmul(bank2(c, BANK_K[l][m])[:, m, 0:T_CTX], wk0[:, k, m * P:(m + 1) * P], ct[c][:, k, 0:T_CTX],
                                           start=k == 0, stop=k == DT - 1)
                        mm.then_inc(k_mm[c], 1)
                else:
                    project(bank2(c, BANK_K[l][0]), l, 1, 0, enc_hi[c], enc_lo[c]).then_inc(k_mm[c], 1)
                    row()
                    project(bank2(c, BANK_K[l][1]), l, 1, 1, enc_hi[c], enc_lo[c]).then_inc(k_mm[c], 1)

            def value_block(c, l, b, bank, half_of_bank):
                t, n = key_blocks(l)[b]
                a_hi, a_lo = (ct_hi, ct_lo) if l == 0 else (enc_hi, enc_lo)
                out = bank2(c, bank)[0:n, half_of_bank, :]
                for k in range(DT):
                    three(out, a_hi[c][:, k, t:t + n], a_lo[c][:, k, t:t + n], w_hi[:, l, 2, k, :], w_lo[:, l, 2, k, :],
                          k == 0, False)
                return pe.matmul(out, ones_r[:, 0:n], bv_split[:, l, :], start=False, stop=True)

            def values_a(c, it, l):
                pe.wait_ge(row_rd[c], nth(it, l))
                value_block(c, l, 0, BANK_VA, 0).then_inc(va_mm[c], 1)

            def values_b(c, it, l):
                if l > 0:
                    pe.wait_ge(p_rd[c], nth(it, l, 2, 2 * HEADS))
                    value_block(c, l, 1, BANK_VB, 0).then_inc(vb_mm[c], 1)

            def scores(c, it, l, s, slots):
                n = T_CTX if l == 0 else S
                for j in slots:
                    h = HEAD_OF_SLOT[j]
                    if s == 0 and h % 2 == 0:
                        pe.wait_ge(k_rd[h // 2][c], nth(it, l))
                    rows = slice(DH * (h % 2), DH * (h % 2) + DH)
                    mm = pe.matmul(bank2(c, 2 * s + j // 2)[:, j % 2, 0:n], qt[c][rows, h // 2, s * P:(s + 1) * P],
                                   kt[c][rows, h // 2, 0:n], start=True, stop=True)
                    if j % 2 == 1:
                        mm.then_inc(sc_mm[c], 1)

            def scores_a(c, it, l):
                pe.wait_ge(q_rd[1][c], nth(it, l))
                if l == 0:
                    pe.wait_ge(kraw_rd[c], nth(it, l, DT, DT))
                scores(c, it, l, 0, ISSUE_ORDER[:-1] if l else ISSUE_ORDER)

            def scores_rest(c, it, l):
                if l > 0:
                    scores(c, it, l, 0, ISSUE_ORDER[-1:])

            def scores_b(c, it, l):
                pe.wait_ge(va_rd[c], nth(it, l))
                scores(c, it, l, 1, ISSUE_ORDER)

            def turn(c, it, l, slots):
                for j in slots:
                    pe.wait_ge(p_rd[c], nth(it, l, HEADS + j + 1, 2 * HEADS))
                    if BANK_OF_TURN[j] == BANK_VB and l > 0:
                        pe.wait_ge(vb_rd[c], nth_vb(it, l))
                    for b, (t, n) in enumerate(key_blocks(l)):
                        for s in range(ST):
                            mm = pe.transpose(bank2(c, BANK_OF_TURN[j])[0:n, b, s * P:(s + 1) * P], prob[c][:, s, j, t:t + n], ident[:])
                    mm.then_inc(pt_mm[c], 1)

            def turn_a(c, it, l):
                turn(c, it, l, TURN_ORDER[:2])

            def turn_b(c, it, l):
                turn(c, it, l, TURN_ORDER[2:])

            def mix(c, it, l):
                if l == 0:
                    pe.wait_ge(vcol_rd[c], nth(it, l))
                blocks = key_blocks(l)
                for s in range(ST):
                    for j in TURN_ORDER:
                        h = HEAD_OF_SLOT[j]
                        if s == 0:
                            pe.wait_ge((ptd_rd, pta_rd)[j % 2][c], nth(it, l, j // 2 + 1, 2))
                        for b, (t, n) in enumerate(blocks):
                            mm = pe.matmul(ps[c][:, BANK_MIX + s, h * VH:(h + 1) * VH], prob_t[c][0:n, j, b, s * P:(s + 1) * P],
                                           v[c][0:n, b, h, :], start=b == 0, stop=b == len(blocks) - 1)
                    mm.then_inc(av_mm[c], 1)

            def norm(c, it, l):
                for s in range(ST):
                    pe.wait_ge(z_rd[c], nth(it, l, s + 1, ST))
                    for m in range(DT):
                        mm = pe.transpose(bank2(c, BANK_ZT)[:, m, s * P:(s + 1) * P], z[c][:, s, m * P:(m + 1) * P], ident[:])
                mm.then_inc(zt_mm[c], 1)

            def feed(c, it, l):
                pe.wait_ge(lnlo_rd[c], nth(it, l, DT, DT))
                for m in range(DT):
                    mm = project(bank2(c, BANK_FF), l, 3, m, ln_hi[c], ln_lo[c])
                mm.then_inc(ff_mm[c], 1)

            steps = dict(align_scores=align_scores, align_turn=align_turn, align_x=align_x, align_out=align_out,
                         natural=natural, queries=queries, keys=keys, values_a=values_a, values_b=values_b, scores_a=scores_a,
                         scores_rest=scores_rest, scores_b=scores_b, turn_a=turn_a, turn_b=turn_b, mix=mix,
                         norm=norm, feed=feed)
            pe.wait_ge(const_in, 64)
            pe.wait_ge(const_rd, 4)
            pe.wait_ge(bias_rd, 3)
            pe.wait_ge(w_split, 2 * (1 + 2 * LAYERS))
            pe.wait_ge(wk0_in, 16)
            run_steps(pe.Fori, lambda name, c, it, l: steps[name](c, it, l) if name in steps else None)

        @block.scalar
        def _(act):
            def col(kind, l, m):
                return cols[:, kind, l, m:m + 1]

            def align_probs(c, it, l):
                act.wait_ge(al_max_rd[c], it + 1)
                for s in range(ST):
                    act.activation(align_e[c][:, s, :], ps[c][:, BANK_AL_SCORES, s * P:s * P + T_CTX], ACT.Exp,
                                   bias=align_nmax[c][:, s:s + 1], accum_out=align_sum[c][:, s:s + 1]).then_inc(al_e_rd[c], 1)
                act.activation(cw[c][0:T_CTX, :], ps[c][0:T_CTX, BANK_AL_SCORES, AL_CW], ACT.Copy).then_inc(cw_rd[c], 1)

            def enc_high(c, it, l):
                for m in range(DT):
                    act.wait_ge(enc_rd[c], nth(it, l, m + 1, DT))
                    act.activation(enc_hi[c][:, m, :], enc_t[c][:, m, :], ACT.Copy).then_inc(enchi_rd[c], 1)

            def align_out(c, it, l):
                for m in range(DT):
                    act.wait_ge(al_x_mm[c], DT * it + m + 1)
                    act.activation(th[c][:, m, :], bank2(c, BANK_AL_X[m])[:, m, :], ACT.Tanh, bias=col(COL_BT, 0, m)).then_inc(th_rd[c], 1)

            def align_encode(c, it, l):
                enc_high(c, it, 0)

            def natural(c, it, l):
                act.wait_ge(nat_mm[c], nth(it, l))
                for s in range(ST):
                    ins = act.activation(enc_n[c][:, s, :], bank2(c, BANK_NATURAL)[:, s, :], ACT.Copy, accum_out=enc_sum[c][:, s:s + 1])
                ins.then_inc(nat_rd[c], 1)

            def queries(c, it, l):
                act.wait_ge(q_mm[c], nth(it, l))
                for m in (range(DT) if l == 0 else (0,)):
                    act.activation(qt[c][:, m, :], bank2(c, BANK_Q)[:, m, :], ACT.Relu, bias=col(COL_BQ, l, m)).then_inc(q_rd[m][c], 1)

            def keys(c, it, l):
                n = T_CTX if l == 0 else S

                def row():
                    act.wait_ge(row_mm[c], nth(it, l))
                    act.activation(keep_row[c][:, 0:n], ps[c][:, BANK_ROW, 0:n], ACT.Copy, accum_out=any_keep[c][:]
                                   ).then_inc(row_rd[c], 1)

                if l == 0:
                    row()
                for m in range(DT):
                    act.wait_ge(k_mm[c], nth(it, l, m + 1 if l else DT, DT))
                    act.activation(kt_raw[c][:, m, 0:n], bank2(c, BANK_K[l][m])[:, m, 0:n], ACT.Relu, bias=bk_scaled[:, l, m:m + 1],
                                   scale=float(DH) ** -0.5).then_inc(kraw_rd[c], 1)
                    if l > 0 and m == 0:
                        row()

            def values_a(c, it, l):
                n = key_blocks(l)[0][1]
                act.wait_ge(keepv_rd[c], nth(it, l))
                act.wait_ge(va_mm[c], nth(it, l))
                act.activation(v[c][0:n, 0, :, 0:DH], bank2(c, BANK_VA)[0:n, 0, :].rearrange("p (h d) -> p h d", h=HEADS), ACT.Relu,
                               scale=keep_v[c][0:n, 0:1]).then_inc(va_rd[c], 1)

            def exps(c, it, l, s):
                n = T_CTX if l == 0 else S
                for j in range(HEADS):
                    if j % 2 == 0:
                        act.wait_ge(max_rd[c], nth(it, l, 2 * s + j // 2 + 1, 2 * ST))
                    act.activation(prob[c][:, s, j, 0:n], bank2(c, 2 * s + j // 2)[:, j % 2, 0:n], ACT.Exp,
                                   bias=nmax[c][:, s, j:j + 1]).then_inc(p_rd[c], 1)

            def scores_b(c, it, l):
                exps(c, it, l, 0)

            def values_b(c, it, l):
                exps(c, it, l, 1)

            def turn(c, it, l, j):
                n, nb = (T_CTX, 1) if l == 0 else (P, ST)
                act.wait_ge(pt_mm[c], nth(it, l, TURN_ORDER.index(j) + 1, HEADS))
                act.activation(prob_t[c][0:n, j, 0:nb, :], bank2(c, BANK_OF_TURN[j])[0:n, 0:nb, :], ACT.Copy).then_inc(pta_rd[c], 1)

            def turn_a(c, it, l):
                turn(c, it, l, 1)

            def turn_b(c, it, l):
                turn(c, it, l, 3)

            def norm(c, it, l):
                act.wait_ge(zt_mm[c], nth(it, l))
                for m in range(DT):
                    act.activation(ln_t[c][:, m, :], bank2(c, BANK_ZT)[:, m, :], ACT.Identity, bias=col(COL_BETA, l, m),
                                   scale=col(COL_GAMMA, l, m)).then_inc(lnt_rd[c], 1)

            def encode(c, it, l):
                if l < LAYERS - 1:
                    enc_high(c, it, l + 1)

            def align_split(c, it, l):
                act.wait_ge(batch_in[c], it * 48 + 48)
                act.wait_ge(al_x_mm[c], DT * it)
                act.activation(xt_hi[c][:], xt[c][:], ACT.Copy).then_inc(x_split[c], 1)

            def feed(c, it, l):
                act.wait_ge(ff_mm[c], nth(it, l))
                for m in range(DT):
                    ins = act.activation(ff[c][:, m, :], bank2(c, BANK_FF)[:, m, :], ACT.Identity, bias=col(COL_BFF, l, m))
                ins.then_inc(u_rd[c], 1)

            steps = dict(align_split=align_split, align_probs=align_probs, align_out=align_out, align_encode=align_encode, natural=natural, keys=keys, queries=queries,
                         values_a=values_a, scores_b=scores_b, values_b=values_b, turn_a=turn_a, turn_b=turn_b,
                         norm=norm, feed=feed, encode=encode)
            act.wait_ge(const_in, 64)
            act.wait_ge(const_rd, 4)
            run_steps(act.Fori, lambda name, c, it, l: steps[name](c, it, l) if name in steps else None)

        @block.gpsimd
        def _(pool):
            def spread(c, it, l):
                pool.wait_ge(var_rd[c], nth(it, l, 2, ST))
                pool.tensor_tensor(std[c][:], var[c][:], half[:], ALU.pow).then_inc(std_rd[c], 1)

            def align_split_low(c, it, l):
                pool.wait_ge(x_split[c], 2 * it + 1)
                pool.tensor_tensor(xt_lo[c][:], xt[c][:], xt_hi[c][:].bitcast(F32), ALU.subtract).then_inc(x_split[c], 1)

            def keys(c, it, l):
                if l == 0:
                    return
                pool.wait_ge(kraw_rd[c], nth(it, l, 2, DT))
                pool.wait_ge(row_rd[c], nth(it, l))
                pool.tensor_tensor(kt[c][:, 1, :], kt_raw[c][:, 1, :], keep_row[c][:], ALU.mult).then_inc(k_rd[1][c], 1)
                if l == LAYERS - 1:
                    pool.wait_ge(out_sent[c], 16 * it)

            def enc_low(c, it, l):
                for m in range(DT):
                    pool.wait_ge(enchi_rd[c], nth(it, l, m + 1, DT))
                    pool.tensor_tensor(enc_lo[c][:, m, :], enc_t[c][:, m, :], enc_hi[c][:, m, :].bitcast(F32), ALU.subtract
                                       ).then_inc(enclo_rd[c], 1)

            def encode(c, it, l):
                last = l == LAYERS - 1
                for m in range(DT):
                    pool.wait_ge(ffl_rd[c], nth(it, l, m + 1, DT))
                    pool.tensor_tensor((final if last else enc_t)[c][:, m, :], ff[c][:, m, :], ln_t[c][:, m, :], ALU.add
                                       ).then_inc((final_rd if last else enc_rd)[c], 1)
                if not last:
                    enc_low(c, it, l + 1)

            def align_out(c, it, l):
                for m in range(DT):
                    pool.wait_ge(th_rd[c], DT * it + m + 1)
                    pool.tensor_tensor(enc_t[c][:, m, :], th[c][:, m, :], xt[c][:, m, :], ALU.add).then_inc(enc_rd[c], 1)

            def align_encode(c, it, l):
                enc_low(c, it, 0)

            pool.wait_ge(const_rd, 4)
            steps = dict(keys=keys, spread=spread, encode=encode, align_split_low=align_split_low, align_out=align_out, align_encode=align_encode)
            run_steps(pool.Fori, lambda name, c, it, l: steps[name](c, it, l) if name in steps else None)

        @block.vector
        def _(dve):
            dve.memset(ones_f[:], 1.0).then_inc(bias_rd, 1)
            dve.memset(half[:], 0.5).then_inc(const_rd, 1)
            for c in CHAINS:
                dve.memset(ct_hi[c][:].bitcast(F32), 0.0).then_inc(pad_rd, 1)
                dve.memset(ct_lo[c][:].bitcast(F32), 0.0).then_inc(pad_rd, 1)
            dve.memset(bv_split[:].bitcast(F32), 0.0).then_inc(pad_rd, 1)
            dve.wait_ge(const_in, 64)
            dve.tensor_copy(ident_bf[:], ident[:]).then_inc(const_rd, 1)
            dve.tensor_scalar(bk_scaled[:], cols[:, COL_BK], float(DH) ** -0.5, None, ALU.mult).then_inc(const_rd, 1)
            dve.wait_ge(bias_rd, 1)
            dve.tensor_copy(ones_r[:], ones_f[:]).then_inc(const_rd, 1)
            dve.tensor_copy(bv_hi[32:33], bv[32:33]).then_inc(pad_rd, 1)
            dve.wait_ge(pad_rd, 6)
            dve.tensor_copy(bv_split[0:1], bv[0:1]).then_inc(bias_rd, 1)
            dve.tensor_tensor(bv_split[32:33], bv[32:33], bv_hi[32:33].bitcast(F32), ALU.subtract).then_inc(bias_rd, 1)
            dests = [(wa_hi[:], wa_lo[:])]
            for l in range(LAYERS):
                for pair in range(2):
                    dests.append(tuple(w[:, l, 2 * pair:2 * pair + 2].rearrange("p w k n -> p (w k) n") for w in (w_hi, w_lo)))
            for n, (hi, lo) in enumerate(dests):
                dve.wait_ge(w_in[n % 2], 16 * (n // 2 + 1))
                dve.tensor_copy(hi, stage_w[:, n % 2]).then_inc(w_split, 1)
                dve.wait_ge(w_split, 2 * n + 1)
                dve.tensor_tensor(lo, stage_w[:, n % 2], hi.bitcast(F32), ALU.subtract).then_inc(w_split, 1)

            def align_split(c, it, l):
                dve.wait_ge(batch_in[c], it * 48 + 48)
                dve.wait_ge(pad_rd, 6)
                if not first_batch(it):
                    dve.wait_ge(va_mm[c], nth(it, 0) - LAYERS)
                dve.tensor_copy(ct_hi[c][:, :, 0:T_CTX], ct[c][:, :, 0:T_CTX]).then_inc(ct_split[c], 1)
                dve.tensor_reduce(c_sum[c][0:T_CTX], cn[c][0:T_CTX, :], AX.X, ALU.add).then_inc(csum_rd[c], 1)
                dve.wait_ge(ct_split[c], 2 * it + 1)
                dve.tensor_tensor(ct_lo[c][:, :, 0:T_CTX], ct[c][:, :, 0:T_CTX], ct_hi[c][:, :, 0:T_CTX].bitcast(F32),
                                  ALU.subtract).then_inc(ct_split[c], 1)

            def align_probs(c, it, l):
                dve.wait_ge(al_sc_mm[c], it + 1)
                dve.tensor_reduce(align_nmax[c][:], ps[c][:, BANK_AL_SCORES, 0:S].rearrange("p (s t) -> p s t", s=ST)[:, :, 0:T_CTX], AX.X,
                                  ALU.max, negate=True).then_inc(al_max_rd[c], 1)
                dve.wait_ge(al_e_rd[c], 2 * it + 2)
                dve.reciprocal(align_rsum[c][:], align_sum[c][:]).then_inc(al_rs_rd[c], 1)
                dve.wait_ge(al_rs_rd[c], it + 1)
                dve.tensor_tensor(align_p[c][:], align_e[c][:], align_rsum[c][:].unsqueeze(2).broadcast_to([P, ST, T_CTX]),
                                  ALU.mult).then_inc(al_p_rd[c], 1)

            def align_out(c, it, l):
                dve.wait_ge(csum_rd[c], it + 1)
                for out in (keep_bf, keep_k):
                    dve.tensor_scalar(out[c][0:T_CTX, 0:1], c_sum[c][0:T_CTX], 0.0, None, ALU.not_equal).then_inc(keepk_rd[c], 1)

            def align_turn(c, it, l):
                dve.wait_ge(al_pt_mm[c], it + 1)
                dve.tensor_copy(align_pt[c][0:T_CTX, :], ps[c][0:T_CTX, BANK_AL_SCORES, 0:S]).then_inc(al_pt_rd[c], 1)

            def natural(c, it, l):
                dve.wait_ge(nat_rd[c], nth(it, l))
                if l > 0:
                    for out in (keep_bf, keep_k):
                        dve.tensor_scalar(out[c][:], enc_sum[c][:], 0.0, None, ALU.not_equal).then_inc(keepk_rd[c], 1)
                dve.tensor_scalar(keep_q[c][:], enc_sum[c][:], 0.0, None, ALU.not_equal).then_inc(keepq_rd[c], 1)

            def queries(c, it, l):
                if l == 0:
                    return
                dve.wait_ge(q_rd[0][c], nth(it, l))
                dve.tensor_scalar(qt[c][:, 1, :], bank2(c, BANK_Q)[:, 1, :], cols[:, COL_BQ, l, 1:2], 0.0, ALU.add, ALU.max
                                  ).then_inc(q_rd[1][c], 1)

            def keys(c, it, l):
                n, nb, keys = (T_CTX, 1, T_CTX) if l == 0 else (P, ST, S)
                dve.wait_ge(row_rd[c], nth(it, l))
                for m in (range(DT) if l == 0 else (0,)):
                    dve.wait_ge(kraw_rd[c], nth(it, l, m + 1, DT))
                    dve.tensor_tensor(kt[c][:, m, 0:keys], kt_raw[c][:, m, 0:keys], keep_row[c][:, 0:keys], ALU.mult
                                      ).then_inc(k_rd[m][c], 1)
                dve.tensor_scalar(none_keep[c][:], any_keep[c][:], 0.0, None, ALU.is_equal).then_inc(none_rd[c], 1)
                dve.wait_ge(none_rd[c], nth(it, l))
                dve.tensor_scalar(keep_v[c][0:n, 0:nb], keep_k[c][0:n, 0:nb], none_keep[c][0:n, 0:1], None,
                                  ALU.max).then_inc(keepv_rd[c], 1)
                dve.wait_ge(keepv_rd[c], nth(it, l))
                dve.tensor_copy(v[c][0:n, 0:nb, :, DH], keep_v[c][0:n, 0:nb].unsqueeze(2).broadcast_to([n, nb, HEADS])
                                ).then_inc(vcol_rd[c], 1)

            def maxes(c, it, l, bank):
                n = T_CTX if l == 0 else S
                dve.wait_ge(sc_mm[c], nth(it, l, bank + 1, 2 * ST))
                dve.tensor_reduce(nmax[c][:, bank // 2, 2 * (bank % 2):2 * (bank % 2) + 2], bank2(c, bank)[:, :, 0:n],
                                  AX.X, ALU.max, negate=True).then_inc(max_rd[c], 1)

            def scores_a(c, it, l):
                maxes(c, it, l, 0)

            def scores_rest(c, it, l):
                maxes(c, it, l, 1)

            def scores_b(c, it, l):
                maxes(c, it, l, 2)

            def values_b(c, it, l):
                maxes(c, it, l, 3)
                if l > 0:
                    dve.wait_ge(vb_mm[c], nth_vb(it, l))
                    dve.tensor_scalar(v[c][:, 1, :, 0:DH], bank2(c, BANK_VB)[:, 0, :].rearrange("p (h d) -> p h d", h=HEADS),
                                      keep_v[c][:, 1:2], 0.0, ALU.mult, ALU.max).then_inc(vb_rd[c], 1)

            def turn(c, it, l, j):
                n, nb = (T_CTX, 1) if l == 0 else (P, ST)
                dve.wait_ge(pt_mm[c], nth(it, l, TURN_ORDER.index(j) + 1, HEADS))
                dve.tensor_copy(prob_t[c][0:n, j, 0:nb, :], bank2(c, BANK_OF_TURN[j])[0:n, 0:nb, :]).then_inc(ptd_rd[c], 1)

            def turn_a(c, it, l):
                turn(c, it, l, 0)

            def turn_b(c, it, l):
                turn(c, it, l, 2)

            def stats(c, it, l, s):
                dve.wait_ge(res_rd[c], nth(it, l, s + 1, ST))
                dve.bn_stats(bn[c][:, s, :], res[c][:, s, :]).then_inc(bn_rd[c], 1)

            def variance(c, it, l, s):
                dve.wait_ge(mv_rd[c], nth(it, l, s + 1, ST))
                dve.tensor_scalar(var[c][:, s:s + 1], mv[c][:, s, 1:2], D / (D - 1.0), None, ALU.mult).then_inc(var_rd[c], 1)

            def mix(c, it, l):
                att_h = att[c][:].rearrange("p s (h d) -> p s h d", h=HEADS)

                def mixed(s):
                    return ps[c][:, BANK_MIX + s, 0:HEADS * VH].rearrange("p (h d) -> p h d", h=HEADS)

                def denominators(s):
                    dve.wait_ge(av_mm[c], nth(it, l, s + 1, ST))
                    dve.reciprocal(rsum[c][:, s], mixed(s)[:, :, DH]).then_inc(rsum_rd[c], 1)

                def factors(s):
                    dve.wait_ge(rsum_rd[c], nth(it, l, s + 1, ST))
                    dve.tensor_scalar(rscale[c][:, s], rsum[c][:, s], keep_q[c][:, s:s + 1], None, ALU.mult).then_inc(rscale_rd[c], 1)

                def attended(s):
                    dve.wait_ge(rscale_rd[c], nth(it, l, s + 1, ST))
                    dve.tensor_tensor(att_h[:, s], mixed(s)[:, :, 0:DH], rscale[c][:, s].unsqueeze(2).broadcast_to([P, HEADS, DH]),
                                      ALU.mult).then_inc(att_rd[c], 1)

                def add_input(s):
                    dve.wait_ge(att_rd[c], nth(it, l, s + 1, ST))
                    dve.tensor_tensor(res[c][:, s, :], att[c][:, s, :], enc_n[c][:, s, :], ALU.add).then_inc(res_rd[c], 1)

                denominators(0)
                dve.wait_ge(keepq_rd[c], nth(it, l))
                factors(0)
                attended(0)
                add_input(0)
                denominators(1)
                stats(c, it, l, 0)
                factors(1)
                attended(1)
                dve.wait_ge(bn_rd[c], nth(it, l, 1, ST))
                add_input(1)
                dve.bn_aggr(mv[c][:, 0, :], bn[c][:, 0, :]).then_inc(mv_rd[c], 1)

            def spread(c, it, l):
                stats(c, it, l, 1)
                dve.wait_ge(bn_rd[c], nth(it, l, 2, ST))
                variance(c, it, l, 0)
                dve.bn_aggr(mv[c][:, 1, :], bn[c][:, 1, :]).then_inc(mv_rd[c], 1)
                variance(c, it, l, 1)

            def center(c, it, l):
                dve.wait_ge(std_rd[c], nth(it, l))
                dve.tensor_scalar(std_eps[c][:], std[c][:], EPS, None, ALU.add).then_inc(stde_rd[c], 1)
                dve.wait_ge(stde_rd[c], nth(it, l))
                dve.reciprocal(rstd[c][:], std_eps[c][:]).then_inc(rstd_rd[c], 1)
                dve.wait_ge(rstd_rd[c], nth(it, l))
                for s in range(ST):
                    dve.tensor_scalar(z[c][:, s, :], res[c][:, s, :], mv[c][:, s, 0:1], rstd[c][:, s:s + 1], ALU.subtract,
                                      ALU.mult).then_inc(z_rd[c], 1)

            def norm_parts(c, it, l):
                for m in range(DT):
                    dve.wait_ge(lnt_rd[c], nth(it, l, m + 1, DT))
                    dve.tensor_copy(ln_hi[c][:, m, :], ln_t[c][:, m, :]).then_inc(lnhi_rd[c], 1)
                for m in range(DT):
                    dve.wait_ge(lnhi_rd[c], nth(it, l, m + 1, DT))
                    dve.tensor_tensor(ln_lo[c][:, m, :], ln_t[c][:, m, :], ln_hi[c][:, m, :].bitcast(F32), ALU.subtract
                                      ).then_inc(lnlo_rd[c], 1)

            def leak(c, it, l):
                dve.wait_ge(u_rd[c], nth(it, l))
                for m in range(DT):
                    dve.scalar_tensor_tensor(ff[c][:, m, :], ff[c][:, m, :], LEAK, ff[c][:, m, :], ALU.mult, ALU.max
                                             ).then_inc(ffl_rd[c], 1)

            steps = dict(align_split=align_split, align_probs=align_probs, align_turn=align_turn, align_out=align_out,
                         natural=natural, queries=queries, keys=keys, spread=spread, values_b=values_b, scores_a=scores_a,
                         scores_rest=scores_rest, scores_b=scores_b, turn_a=turn_a, turn_b=turn_b, mix=mix,
                         center=center, norm_parts=norm_parts, leak=leak)
            run_steps(dve.Fori, lambda name, c, it, l: steps[name](c, it, l) if name in steps else None)


def columns_of(vectors):
    n, layers, d = vectors.shape
    return np.ascontiguousarray(vectors.reshape(n, layers, d // P, P).transpose(3, 0, 1, 2))


def kernel(**inputs):
    import concourse.bacc as bacc
    from concourse.bass_utils import run_bass_kernel_spmd

    a = {k: np.asarray(x) for k, x in inputs.items()}
    bt = a["L0_xattn_trans_b"]
    arrays = {
        "x_t": np.ascontiguousarray(a["x"].transpose(0, 2, 1)),
        "ctx_t": np.ascontiguousarray(a["ctx_1024"].transpose(0, 2, 1)),
        "ctx_n": np.ascontiguousarray(a["ctx_1024"]),
        "w_align": np.ascontiguousarray(a["L0_xattn_trans_W"]),
        "w_qkvf": np.ascontiguousarray(np.stack([a["L1_xattn_Wq"], a["L1_xattn_Wk"], a["L1_xattn_Wv"], a["L1_xattn_Wff"]], 1)),
        "columns": columns_of(np.stack([a["L1_xattn_bq"], a["L1_xattn_bk"], a["L1_xattn_gamma"], a["L1_xattn_beta"],
                                        a["L1_xattn_bff"], np.stack([bt] * LAYERS)])),
        "bv_row": np.ascontiguousarray(a["L1_xattn_bv"][None]),
        "identity": np.eye(P, dtype=np.float32),
    }
    nc = bacc.Bacc("TRN2", target_bir_lowering=False, num_devices=1)
    aps = [nc.dram_tensor(f"in_{n}", x.shape, mybir.dt.from_np(x.dtype), kind="ExternalInput").ap() for n, x in arrays.items()]
    b, s, d = a["x"].shape
    out = nc.dram_tensor("out_t", (b, d, s), F32, kind="ExternalOutput").ap()
    build_program(nc, *aps, out)
    r = run_bass_kernel_spmd(nc, [{f"in_{n}": x for n, x in arrays.items()}], core_ids=[0])
    return np.ascontiguousarray(r.results[0]["out_t"].transpose(0, 2, 1))
```
